# Optimizing a Trainium2 kernel written in Bass

```python
import numpy as np
import jax
import jax.numpy as jnp

def _softmax(x, axis=-1):
    return jax.nn.softmax(x, axis=axis)

def _gelu(x):
    return jax.nn.gelu(x, approximate=True)

def _silu(x):
    return jax.nn.silu(x)

def _sigmoid(x):
    return jax.nn.sigmoid(x)

def _layernorm(x, axis=-1, eps=1e-05):
    m = jnp.mean(x, axis=axis, keepdims=True)
    v = jnp.var(x, axis=axis, keepdims=True)
    return (x - m) / jnp.sqrt(v + eps)

def _scatter_add(tgt, idx, src, axis=0):
    return tgt.at[idx].add(src)

def _segment_sum(src, seg, n):
    return jax.ops.segment_sum(src, seg, n)
kernel_name = 'mk_adaln_d1_jaxref_r4_592ea4'

def setup_inputs(seed: int=0):
    np.random.seed(seed)
    _w = jnp.asarray

    def _L0_attn_setup():
        import jax, jax.numpy as jnp
        import numpy as np
        B, S, D = (2, 512, 256)
        H, DH = (16, 64)
        DQL, DKVL = (128, 128)
        DR = 64
        TOPK = 64
        LN_EPS = 1e-05
        ROPE_BASE = 10000.0

        def _rope_tables(seq_len, dim):
            inv_freq = 1.0 / ROPE_BASE ** (np.arange(0, dim, 2, dtype=np.float32) / dim)
            t = np.arange(seq_len, dtype=np.float32)
            freqs = np.outer(t, inv_freq)
            cos = np.concatenate([np.cos(freqs), np.cos(freqs)], -1)[:, ::2]
            sin = np.concatenate([np.sin(freqs), np.sin(freqs)], -1)[:, ::2]
            return (jnp.asarray(cos), jnp.asarray(sin))

        def _apply_rope_subspace(x, d_rope):
            s = x.shape[-2]
            cos, sin = _rope_tables(s, d_rope)
            xr, xp = (x[..., :d_rope], x[..., d_rope:])
            e, o = (xr[..., 0::2], xr[..., 1::2])
            rot = jnp.stack([e * cos - o * sin, e * sin + o * cos], axis=-1).reshape(xr.shape)
            return jnp.concatenate([rot, xp], axis=-1)

        def _reference_tuple_inner(x, w_down_q, w_down_kv, w_up_q, w_up_k, w_up_v, w_out, ln_scale, ln_bias):
            b, s, d = x.shape
            residual = x
            mu = jnp.mean(x, axis=-1, keepdims=True)
            var = jnp.mean((x - mu) ** 2, axis=-1, keepdims=True)
            h = (x - mu) * jax.lax.rsqrt(var + LN_EPS) * ln_scale + ln_bias
            c_q = h @ w_down_q.T
            c_kv = h @ w_down_kv.T
            q = (c_q @ w_up_q.T).reshape(b, s, H, DH).transpose(0, 2, 1, 3)
            k = (c_kv @ w_up_k.T).reshape(b, s, H, DH).transpose(0, 2, 1, 3)
            v = (c_kv @ w_up_v.T).reshape(b, s, H, DH).transpose(0, 2, 1, 3)
            q = _apply_rope_subspace(q, DR)
            k = _apply_rope_subspace(k, DR)
            scale = 1.0 / np.sqrt(DH).astype(np.float32)
            scores = jnp.einsum('bhqd,bhkd->bhqk', q, k) * scale
            _, indices = jax.lax.top_k(scores, min(TOPK, s))
            attn = jax.nn.softmax(scores, axis=-1)
            out = jnp.einsum('bhqk,bhkd->bhqd', attn, v)
            out = out.transpose(0, 2, 1, 3).reshape(b, s, H * DH)
            out = out @ w_out.T + residual
            return (out, indices.astype(jnp.int64))
        key = jax.random.key(seed)
        ks = jax.random.split(key, 7)
        init = lambda k, shape: jax.random.normal(k, shape, jnp.float32) * 0.02
        return {'x': jax.random.normal(ks[0], (B, S, D), jnp.float32), 'w_down_q': init(ks[1], (DQL, D)), 'w_down_kv': init(ks[2], (DKVL, D)), 'w_up_q': init(ks[3], (H * DH, DQL)), 'w_up_k': init(ks[4], (H * DH, DKVL)), 'w_up_v': init(ks[5], (H * DH, DKVL)), 'w_out': init(ks[6], (D, H * DH)), 'ln_scale': jnp.ones((D,), jnp.float32), 'ln_bias': jnp.zeros((D,), jnp.float32)}
    _L0_attn_in = _L0_attn_setup()

    def _L0_ffn_setup():
        import jax, jax.numpy as jnp
        import numpy as np
        LORA_DIM = 16
        LORA_TOKEN_INDEX = 1
        B, S, D, H = (4, 512, 256, 1024)
        key = jax.random.key(seed)
        ks = jax.random.split(key, 6)
        x = jax.random.normal(ks[0], (B, S, D), dtype=jnp.float32)
        W1 = jax.random.normal(ks[1], (H, D), dtype=jnp.float32) * 0.02
        b1 = jnp.zeros((H,), dtype=jnp.float32)
        W2 = jax.random.normal(ks[2], (D, H), dtype=jnp.float32) * 0.02
        b2 = jnp.zeros((D,), dtype=jnp.float32)
        scale = jnp.asarray(0.001, dtype=jnp.float32)
        return {'x': x, 'W1': W1, 'b1': b1, 'W2': W2, 'b2': b2, 'scale': scale}
    _L0_ffn_in = _L0_ffn_setup()
    _L0_c = _w((lambda *s: np.random.randn(*s).astype(np.float32) * 0.05)(8, 256))
    _L0_wmod = _w((lambda *s: np.random.randn(*s).astype(np.float32) * 0.05)(256, 6 * 256) * 256 ** (-0.5))
    _d = {'L0_attn_x': _L0_attn_in['x'], 'L0_attn_w_down_q': _L0_attn_in['w_down_q'], 'L0_attn_w_down_kv': _L0_attn_in['w_down_kv'], 'L0_attn_w_up_q': _L0_attn_in['w_up_q'], 'L0_attn_w_up_k': _L0_attn_in['w_up_k'], 'L0_attn_w_up_v': _L0_attn_in['w_up_v'], 'L0_attn_w_out': _L0_attn_in['w_out'], 'L0_attn_ln_scale': _L0_attn_in['ln_scale'], 'L0_attn_ln_bias': _L0_attn_in['ln_bias'], 'L0_ffn_W1': _L0_ffn_in['W1'], 'L0_ffn_b1': _L0_ffn_in['b1'], 'L0_ffn_W2': _L0_ffn_in['W2'], 'L0_ffn_b2': _L0_ffn_in['b2'], 'L0_ffn_scale': _L0_ffn_in['scale'], 'L0_c': _L0_c, 'L0_wmod': _L0_wmod}
    _x0 = _d['L0_attn_x']
    _d['L0_attn_x'] = jax.random.normal(jax.random.fold_in(jax.random.key(seed), 1), (8, 1024, 256), dtype=_x0.dtype)
    del _x0
    return _d

def reference(L0_attn_x, L0_attn_w_down_q, L0_attn_w_down_kv, L0_attn_w_up_q, L0_attn_w_up_k, L0_attn_w_up_v, L0_attn_w_out, L0_attn_ln_scale, L0_attn_ln_bias, L0_ffn_W1, L0_ffn_b1, L0_ffn_W2, L0_ffn_b2, L0_ffn_scale, L0_c, L0_wmod):

    def _L0_attn_ref(x, w_down_q, w_down_kv, w_up_q, w_up_k, w_up_v, w_out, ln_scale, ln_bias):
        import jax, jax.numpy as jnp
        import numpy as np
        B, S, D = (2, 512, 256)
        H, DH = (16, 64)
        DQL, DKVL = (128, 128)
        DR = 64
        TOPK = 64
        LN_EPS = 1e-05
        ROPE_BASE = 10000.0

        def _rope_tables(seq_len, dim):
            inv_freq = 1.0 / ROPE_BASE ** (np.arange(0, dim, 2, dtype=np.float32) / dim)
            t = np.arange(seq_len, dtype=np.float32)
            freqs = np.outer(t, inv_freq)
            cos = np.concatenate([np.cos(freqs), np.cos(freqs)], -1)[:, ::2]
            sin = np.concatenate([np.sin(freqs), np.sin(freqs)], -1)[:, ::2]
            return (jnp.asarray(cos), jnp.asarray(sin))

        def _apply_rope_subspace(x, d_rope):
            s = x.shape[-2]
            cos, sin = _rope_tables(s, d_rope)
            xr, xp = (x[..., :d_rope], x[..., d_rope:])
            e, o = (xr[..., 0::2], xr[..., 1::2])
            rot = jnp.stack([e * cos - o * sin, e * sin + o * cos], axis=-1).reshape(xr.shape)
            return jnp.concatenate([rot, xp], axis=-1)

        def _reference_tuple_inner(x, w_down_q, w_down_kv, w_up_q, w_up_k, w_up_v, w_out, ln_scale, ln_bias):
            b, s, d = x.shape
            residual = x
            mu = jnp.mean(x, axis=-1, keepdims=True)
            var = jnp.mean((x - mu) ** 2, axis=-1, keepdims=True)
            h = (x - mu) * jax.lax.rsqrt(var + LN_EPS) * ln_scale + ln_bias
            c_q = h @ w_down_q.T
            c_kv = h @ w_down_kv.T
            q = (c_q @ w_up_q.T).reshape(b, s, H, DH).transpose(0, 2, 1, 3)
            k = (c_kv @ w_up_k.T).reshape(b, s, H, DH).transpose(0, 2, 1, 3)
            v = (c_kv @ w_up_v.T).reshape(b, s, H, DH).transpose(0, 2, 1, 3)
            q = _apply_rope_subspace(q, DR)
            k = _apply_rope_subspace(k, DR)
            scale = 1.0 / np.sqrt(DH).astype(np.float32)
            scores = jnp.einsum('bhqd,bhkd->bhqk', q, k) * scale
            _, indices = jax.lax.top_k(scores, min(TOPK, s))
            attn = jax.nn.softmax(scores, axis=-1)
            out = jnp.einsum('bhqk,bhkd->bhqd', attn, v)
            out = out.transpose(0, 2, 1, 3).reshape(b, s, H * DH)
            out = out @ w_out.T + residual
            return (out, indices.astype(jnp.int64))
        return _reference_tuple_inner(x, w_down_q, w_down_kv, w_up_q, w_up_k, w_up_v, w_out, ln_scale, ln_bias)[0]

    def _L0_ffn_ref(x, W1, b1, W2, b2, scale):
        import jax, jax.numpy as jnp
        import numpy as np
        LORA_DIM = 16
        LORA_TOKEN_INDEX = 1
        B, S, D, H = (4, 512, 256, 1024)
        Bx, Sx, Dx = x.shape
        Hx = W1.shape[0]
        lt = jax.lax.dynamic_slice_in_dim(x, LORA_TOKEN_INDEX, LORA_DIM, axis=1)
        even = lt[:, ::2, :]
        odd = lt[:, 1::2, :]
        m1 = (even[:, :4, :, None] * odd[:, :4, None, :]).reshape(Bx, Hx, Dx)
        m2 = (even[:, 4:, :, None] * odd[:, 4:, None, :]).reshape(Bx, Dx, Hx)
        h = jnp.einsum('bsd,hd->bsh', x, W1) + scale * jnp.einsum('bsd,bhd->bsh', x, m1) + b1
        h = jax.nn.gelu(h, approximate=False)
        out = jnp.einsum('bsh,oh->bso', h, W2) + scale * jnp.einsum('bsh,boh->bso', h, m2) + b2
        return out
    x = L0_attn_x
    mod = (_silu(L0_c) @ L0_wmod).reshape(L0_c.shape[0], 6, 1, -1)
    sa, ca, ga, sb, cb, gb = (mod[:, 0], mod[:, 1], mod[:, 2], mod[:, 3], mod[:, 4], mod[:, 5])
    ga = (2 * (ga >= 0) - 1) * jnp.maximum(jnp.abs(ga), 0.25)
    gb = (2 * (gb >= 0) - 1) * jnp.maximum(jnp.abs(gb), 0.25)
    h = _layernorm(x, axis=-1) * (1 + ca) + sa
    x = x + ga * _L0_attn_ref(h, L0_attn_w_down_q, L0_attn_w_down_kv, L0_attn_w_up_q, L0_attn_w_up_k, L0_attn_w_up_v, L0_attn_w_out, L0_attn_ln_scale, L0_attn_ln_bias)
    h = _layernorm(x, axis=-1) * (1 + cb) + sb
    x = x + gb * _L0_ffn_ref(h, L0_ffn_W1, L0_ffn_b1, L0_ffn_W2, L0_ffn_b2, L0_ffn_scale)
    return x

_drawn_inputs = setup_inputs


def setup_inputs(seed=0):
    import zlib

    import numpy as np

    out = dict(_drawn_inputs(seed))
    spreads = {'L0_attn_ln_scale': (1.0, 0.6),
     'L0_attn_ln_bias': (0.0, 0.8),
     'L0_ffn_b1': (0.0, 2.0),
     'L0_ffn_b2': (0.0, 2.0)}
    factors = {'L0_attn_w_down_q': 8.0,
     'L0_attn_w_down_kv': 8.0,
     'L0_attn_w_up_q': 8.0,
     'L0_attn_w_up_k': 8.0,
     'L0_attn_w_up_v': 8.0,
     'L0_attn_w_out': 8.0,
     'L0_ffn_W1': 8.0,
     'L0_ffn_W2': 5.784}
    for name, (base, spread) in spreads.items():
        noise = np.random.default_rng([zlib.crc32(name.encode()), seed]).standard_normal(out[name].shape)
        drawn = base * np.exp(spread * noise) if base else spread * noise
        out[name] = jnp.asarray(drawn.astype(out[name].dtype))
    for name, factor in factors.items():
        out[name] = (out[name] * factor).astype(out[name].dtype)
    return out
```

```python
from contextlib import ExitStack

import concourse.bass as bass
from concourse import mybir

B, S, D = 8, 1024, 256
H, DH = 16, 64
R = 128
HID = 1024
P = 128
NP = H // 2
NT = S // P
KD = D // P
NH = HID // P
HALF = 512
NHALF = S // HALF
TPH = HALF // P
LORA = 4
EPS = 1e-5
SCALE = DH ** -0.5

M_RING = 3
M_PROJ, M_SUM, M_MAX, M_ROW = 8, 2, 4 * NT, 2
M_PREP = M_PROJ + M_MAX + M_ROW
M_STEP = M_PREP + M_SUM
M_A = 4 + NT
M_PREP0 = M_A
M_STEP0 = M_PREP0 + M_PREP
M_STEP1 = M_STEP0 + M_PREP
M_LAST = M_STEP1 + (NP - 2) * M_STEP
M_FIN = M_LAST + M_SUM
M_C = M_FIN + M_SUM
M_OUT, M_LORA, M_FFN2 = NT // 2, 4, NT // 2
M_ALL = M_C + M_OUT + M_LORA + M_FFN2
T_RING = 3
T_TR = 4
T_A = T_TR + NT
T_PAIR = 4 * NT
T_C = T_A + NP * T_PAIR
T_ALL = T_C + T_TR + 2 * NH
P_RING = 8
ADDS = 4 * (NT - 1)
PV = 2 * NT


def step_base(p):
    return M_STEP1 + (p - 1) * M_STEP


def build(nc, x, w_pair, w_v, w_down, w_out, w1, w2, ln_cols, b1_cols, b2, lora_scale,
          c_cols, w_mod, rope, ident_in, diag_in, out):
    f32, f32r = mybir.dt.float32, mybir.dt.float32r
    ALU, ACT, AX = mybir.AluOpType, mybir.ActivationFunctionType, mybir.AxisListType

    mod_d = nc.dram_tensor("mod_rows", [B, 6 * D], f32, kind="Internal").ap()
    inv_d = nc.dram_tensor("inverse_sums", [2, S], f32, kind="Internal").ap()

    ctx = ExitStack()
    with ctx:
        def sb(name, shape, dt=f32, stack=ctx):
            return stack.enter_context(nc.sbuf_tensor(name, shape, dt))

        def sem(name):
            return ctx.enter_context(nc.semaphore(name))

        ident = sb("ident", [P, P])
        ones = sb("ones", [P, P])
        diag = sb("diag", [NT, NT])
        neg_half = sb("neg_half", [P, NT])
        ln_t = sb("ln_t", [P, 2 * KD])
        b1_t = sb("b1_t", [P, NH])
        b2_bc = sb("b2_bc", [P, D])
        ls_bc = sb("ls_bc", [P, 1])
        mod_t = sb("mod_t", [P, 2 * KD, B])
        mod_c = sb("mod_c", [P, 2 * KD, 1])
        cos_sin = sb("cos_sin", [P, 2, S])
        wo = sb("wo", [P, NP, D])
        mod_bc = sb("mod_bc", [P, 4, D])
        xres = sb("xres", [P, NT, D])
        cT = sb("cT", [P, 2, S])
        VS = sb("VS", [P, NP, S])
        wp = [sb(f"wp{u}", [P, 4, P]) for u in range(2)]
        sums = sb("sums", [P, S])
        rb = sb("rb", [P, S])
        cs = sb("cs", [P, 2, NT])
        rc = sb("rc", [P, 2, NT])
        stats = sb("stats", [P, NT, 6])
        mv = sb("mv", [P, NT, 2])
        ve = sb("ve", [P, NT])
        rstd = sb("rstd", [P, NT])
        mxp = sb("mxp", [P, 2 * NT, 2])
        mx = sb("mx", [P, 2 * NT])
        sodd = sb("sodd", [P, KD, 2 * LORA])
        T2m = [[sb(f"T2m{u}{h}", [P, S], f32r) for h in range(2)] for u in range(2)]
        T2s = [[sb(f"T2s{u}{h}", [P, S], f32r) for h in range(2)] for u in range(2)]

        def shared(*layouts):
            made = []
            for n, layout in enumerate(layouts):
                stack = ctx if n == len(layouts) - 1 else ExitStack()
                made += [sb(name, shape, dt, stack) for name, shape, dt in layout]
                if n < len(layouts) - 1:
                    stack.close()
            return made

        xt, hbuf, nbuf, hT, hid, *t1 = shared(
            [("xt", [P, NT, D], f32), ("hbuf", [P, NT, D], f32), ("nbuf", [P, NT, D], f32),
             ("hT", [P, KD, S], f32)],
            [("hid", [P, NH, S], f32)],
            [(f"T1{k}{u}{h}", [P, S], f32r) for k in "ms" for u in range(2) for h in range(2)])
        T1m, T1s = [t1[0:2], t1[2:4]], [t1[4:6], t1[6:8]]
        w1_sb, w2_sb, Pt = shared(
            [("w1_sb", [P, KD, HID], f32), ("w2_sb", [P, NH, D], f32)],
            [("Pt", [P, P_RING, HALF], f32)])
        n2buf, D_sb, acc = shared(
            [("n2buf", [P, NT, D], f32), ("D_sb", [P, KD, 2 * LORA, P], f32)],
            [("acc", [P, 2, 2, S], f32)])
        h3T, Vp0, Vp1 = shared([("h3T", [P, KD, S], f32)],
                               [("Vp0", [P, NT, P], f32), ("Vp1", [P, NT, P], f32)])
        Vp = [Vp0, Vp1]
        wd, wv, rot = shared([("wd", [P, KD, 2, R], f32), ("wv", [P, H * DH], f32)],
                             [("rot", [P, 2, S], f32)])
        obuf, tmp = shared([("obuf", [P, 2, 2, D], f32)], [("tmp", [P, 2, HALF], f32)])
        c_sb, e_c, silu_c = (sb(n, [P, KD * B]) for n in ("c_sb", "e_c", "silu_c"))
        wm = VS[:, 0:3, :].rearrange("p a s -> p (a s)").rearrange("p (k n) -> p k n", k=KD)
        modr = VS[0:B, 3:5, :].rearrange("p a s -> p (a s)")[:, 0:6 * D]
        guard = VS[0:B, 5, :].rearrange("p (k d) -> p k d", d=D)

        MB = [ctx.enter_context(nc.psum_tensor(f"M{i}", [P, HALF], f32)) for i in range(M_RING)]
        TB = [ctx.enter_context(nc.psum_tensor(f"T{i}", [P, HALF], f32)) for i in range(T_RING)]
        OB = [ctx.enter_context(nc.psum_tensor(f"O{i}", [P, HALF], f32)) for i in range(2)]

        const_in = sem("const_in")
        const_set = sem("const_set")
        setup = sem("setup")
        exp_c, silu_done = sem("exp_c"), sem("silu_done")
        mod_mm = sem("mod_mm")
        rows_done = sem("rows_done")
        m_ready = sem("m_ready")
        m_used = sem("m_used")
        t_ready = sem("t_ready")
        t_used = sem("t_used")
        rope_done = sem("rope_done")
        hi_done = sem("hi_done")
        lo_done = sem("lo_done")
        max_done = sem("max_done")
        pv_done = sem("pv_done")
        add_done = sem("add_done")
        o_used = sem("o_used")
        inv_done = sem("inv_done")
        norm_done = sem("norm_done")
        x_in = sem("x_in")
        wa_in = sem("wa_in")
        wc_in = sem("wc_in")
        wp_in = [sem(f"wp_in{u}") for u in range(2)]
        v_in = [sem(f"v_in{u}") for u in range(2)]
        cs_in, inv_out, rb_in = sem("cs_in"), sem("inv_out"), sem("rb_in")
        stats_done, merged, var_done = sem("stats_done"), sem("merged"), sem("var_done")
        rstd_done = sem("rstd_done")
        normed = sem("normed")
        modulated = sem("modulated")
        cols_done = sem("cols_done")
        x1_done = sem("x1_done")
        odd_done, spread_done = sem("odd_done"), sem("spread_done")
        gated = sem("gated")
        out_ready = sem("out_ready")
        stored = [sem(f"stored{i}") for i in range(2)]

        LOADS = 10

        block = ctx.enter_context(nc.Block())

        def steps(eng, b, step):
            step(8 * b, 0, 0, True, False)
            with eng.Fori(0, (NP - 2) // 2) as i:
                for r in (1, 2):
                    step(8 * b + (2 * i + r), 2 * i + r, r % 2, True, True)
            step(8 * b + NP - 1, NP - 1, (NP - 1) % 2, False, True)

        def m_base(b, p):
            if isinstance(p, int) and p == 0:
                return b * M_ALL + M_STEP0
            return b * M_ALL + step_base(p)

        def t_base(b, p):
            return b * T_ALL + T_A + p * T_PAIR

        @block.sync
        def _(sp):
            for dst, src in ((ident[:, :], ident_in), (diag[:, :], diag_in), (ln_t[:, :], ln_cols),
                             (b1_t[:, :], b1_cols), (b2_bc[:, :], b2.partition_broadcast(P)),
                             (ls_bc[:, :], lora_scale.partition_broadcast(P)),
                             (c_sb[:, :], c_cols), (wm, w_mod),
                             (cos_sin[:, :, :], rope), (wo[:, :, :], w_out)):
                sp.dma_start(dst, src).then_inc(const_in, 16)
            sp.wait_ge(rows_done, 3)
            for i in range(2):
                half = slice(i * B // 2, (i + 1) * B // 2)
                sp.dma_start(mod_d[half, :], modr[half, :]).then_inc(stored[i], 16)
            for i in range(2):
                sp.wait_ge(stored[i], 16)

            def finish(g, m_sums, prev):
                sp.wait_ge(m_used, m_sums)
                for h in range(2):
                    sp.dma_start(cs[:, h, :], sums[64 * h:64 * h + 1, :]).then_inc(cs_in, 16)
                sp.wait_ge(inv_done, g)
                for h in range(2):
                    sp.dma_start(inv_d[h, :].rearrange("(p j) -> p j", p=P), rc[:, h, :]).then_inc(inv_out, 16)
                sp.wait_ge(inv_out, 32 * g)
                for h in range(2):
                    sp.dma_start(rb[64 * h:64 * h + 64, :], inv_d[h:h + 1, :].partition_broadcast(64))\
                        .then_inc(rb_in, 16)

            with sp.Fori(0, B) as b:
                sp.dma_start(xt[:, :, :], x[bass.ds(b, 1), :, :].rearrange("a (t p) d -> p (a t) d", p=P))\
                    .then_inc(x_in, 16)
                for j, m in enumerate((0, 1, 2, 5)):
                    sp.dma_start(mod_bc[:, j:j + 1, :],
                                 mod_d[bass.ds(b, 1), m * D:(m + 1) * D].partition_broadcast(P))\
                        .then_inc(x_in, 16)
                sp.dma_start(wd[:, :, :, :], w_down).then_inc(wa_in, 16)
                sp.dma_start(wv[:, :], w_v).then_inc(wa_in, 16)
                sp.dma_start(wp[0][:, :, :], w_pair[0]).then_inc(wp_in[0], 16)
                sp.wait_ge(m_used, b * M_ALL + M_A)
                sp.wait_ge(t_used, b * T_ALL + T_A)
                sp.dma_start(Vp[0][:, :, :], VS[:, 0, :]).then_inc(v_in[0], 16)

                def step(g, p, u, prep, fin):
                    if prep:
                        if fin:
                            sp.wait_ge(pv_done, PV * g - PV + 1)
                        sp.dma_start(wp[1 - u][:, :, :], w_pair[bass.ds(p + 1, 1), :, :, :]
                                     .rearrange("a p k n -> p (a k) n")).then_inc(wp_in[1 - u], 16)
                        if fin:
                            sp.wait_ge(pv_done, PV * g)
                        sp.dma_start(Vp[1 - u][:, :, :], VS[:, bass.ds(p + 1, 1), :]).then_inc(v_in[1 - u], 16)
                    if fin:
                        finish(g, m_base(b, p) + (M_PROJ if prep else 0) + M_SUM, p - 1)

                steps(sp, b, step)
                sp.wait_ge(pv_done, PV * 8 * b + PV * NP)
                sp.wait_ge(add_done, ADDS * 8 * b + ADDS * NP)
                sp.dma_start(w1_sb[:, :, :], w1).then_inc(wc_in, 16)
                sp.dma_start(w2_sb[:, :, :], w2).then_inc(wc_in, 16)
                finish(8 * b + NP, b * M_ALL + M_C, NP - 1)
                for w in range(M_FFN2):
                    sp.wait_ge(out_ready, 4 * b + w + 1)
                    sp.dma_start(out[bass.ds(b, 1), 2 * w * P:2 * (w + 1) * P, :]
                                 .rearrange("a (t p) d -> p (a t) d", p=P), obuf[:, w % 2, :, :])\
                        .then_inc(stored[w % 2], 16)
            for i in range(2):
                sp.wait_ge(stored[i], 16 + 32 * B)

        @block.tensor
        def _(pe):
            pe.wait_ge(const_in, 16 * LOADS)
            pe.wait_ge(silu_done, 1)
            for n in range(3):
                for k in range(KD):
                    mm = pe.matmul(MB[n][0:B, :], silu_c[:, k * B:(k + 1) * B],
                                   wm[:, k, n * HALF:(n + 1) * HALF], start=(k == 0), stop=(k == KD - 1))
            for j in range(2 * KD):
                for k in range(KD):
                    mm = pe.matmul(TB[0][:, j * B:(j + 1) * B], wm[:, k, 3 * D + j * P:3 * D + (j + 1) * P],
                                   silu_c[:, k * B:(k + 1) * B], start=(k == 0), stop=(k == KD - 1))
            mm.then_inc(mod_mm, 1)
            pe.wait_ge(const_set, 14)
            pe.wait_ge(rows_done, 3)

            with pe.Fori(0, B) as b:
                def m_bank(base, j):
                    pe.wait_ge(m_used, base if j < M_RING else base + (j - M_RING + 1))
                    return MB[j % M_RING]

                def t_bank(base, j):
                    pe.wait_ge(t_used, base if j < T_RING else base + (j - T_RING + 1))
                    return TB[j % T_RING]

                def bank_a(which, base, j):
                    if j >= 3:
                        pe.wait_ge(m_used if which is MB else t_used, base + (j - 2))
                    return which[j % 3]

                def transposes(bank, j, src):
                    k, half = j // NHALF, j % NHALF
                    for c in range(TPH):
                        mm = pe.transpose(bank[:, c * P:(c + 1) * P],
                                          src[:, TPH * half + c, k * P:(k + 1) * P], ident[:, :])
                    mm.then_inc(t_ready, 1)

                ma, ta = b * M_ALL, b * T_ALL
                pe.wait_ge(normed, 3 * NT * b + 2 * NT)
                for j in range(T_TR):
                    transposes(bank_a(TB, ta, j), j, nbuf)
                pe.wait_ge(wa_in, 32 * b + 32)
                pe.wait_ge(t_used, ta + T_TR)
                for j in range(4):
                    kind, half = j // 2, j % 2
                    bank = bank_a(MB, ma, j)
                    for k in range(KD):
                        mm = pe.matmul(bank[:, :], wd[:, k, kind, :], hT[:, k, half * HALF:(half + 1) * HALF],
                                       start=(k == 0), stop=(k == KD - 1))
                    mm.then_inc(m_ready, 1)
                pe.wait_ge(m_used, ma + 4)
                for t in range(NT):
                    for f in range(2):
                        bank = bank_a(MB, ma, 4 + t) if f == 0 else bank_a(TB, ta, T_TR + t)
                        pe.matmul(bank[:, :], cT[:, 1, t * P:(t + 1) * P], wv[:, f * HALF:(f + 1) * HALF],
                                  start=True, stop=True).then_inc(m_ready if f == 0 else t_ready, 1)

                def proj(base, j, g, u):
                    if j == 0:
                        pe.wait_ge(wp_in[u], 8 * (g - u) + 16)
                    kind, half, swap = j // 4, j // 2 % 2, j % 2
                    pe.matmul(m_bank(base, j)[:, :], wp[u][:, 2 * kind + swap, :],
                              cT[:, kind, half * HALF:(half + 1) * HALF],
                              start=True, stop=True).then_inc(m_ready, 1)

                def scores_max(base, j, n, g, u):
                    if n == 0:
                        pe.wait_ge(hi_done, 8 * g + 8)
                        pe.wait_ge(lo_done, 4 * g + 2)
                    h, t, half = n // (2 * NT), n // 2 % NT, n % 2
                    pe.matmul(m_bank(base, j)[:, :], T1m[u][h][:, t * P:(t + 1) * P],
                              T1s[u][h][:, half * HALF:(half + 1) * HALF],
                              start=True, stop=True).then_inc(m_ready, 1)

                def max_rows(base, j, h, g):
                    pe.wait_ge(max_done, g + 1)
                    pe.transpose(m_bank(base, j)[0:NT, 0:P], mx[:, h * NT:(h + 1) * NT], ident[:, :])\
                        .then_inc(m_ready, 1)

                def sum_rows(base, j, half, g, u):
                    pe.wait_ge(add_done, ADDS * g + ADDS)
                    bank = m_bank(base, j)
                    for h in range(2):
                        mm = pe.matmul(bank[64 * h:64 * h + 64, :], ones[:, 0:64],
                                       acc[:, u, h, half * HALF:(half + 1) * HALF], start=True, stop=True)
                    mm.then_inc(m_ready, 1)

                base = b * M_ALL + M_PREP0
                for j in range(M_PROJ):
                    proj(base, j, 8 * b, 0)
                for n in range(M_MAX):
                    scores_max(base, M_PROJ + n, n, 8 * b, 0)
                for h in range(2):
                    max_rows(base, M_PROJ + M_MAX + h, h, 8 * b)

                def step(g, p, u, prep, fin):
                    mb, tb = m_base(b, p), t_base(b, p)
                    work = []
                    if prep:
                        work += [(2 + n // 2, proj, (mb, n, g + 1, 1 - u)) for n in range(M_PROJ)]
                    n0 = M_PROJ if prep else 0
                    if fin:
                        work += [(6, sum_rows, (mb, n0 + n, n, g - 1, 1 - u)) for n in range(M_SUM)]
                        n0 += M_SUM
                    if prep:
                        work += [(8 + n // 4, scores_max, (mb, n0 + n, n, g + 1, 1 - u)) for n in range(M_MAX)]

                    def values(i):
                        half, k = i // NT, i % NT
                        pe.wait_ge(t_used, tb + 2 * i + 2)
                        if k == 0 and fin:
                            pe.wait_ge(o_used, 2 * g - 1 + half)
                        for h in range(2):
                            mm = pe.matmul(OB[half][64 * h:64 * h + 64, :], Vp[u][:, k, 64 * h:64 * h + 64],
                                           Pt[:, (2 * i + h) % P_RING, :], start=(k == 0), stop=(k == NT - 1))
                        mm.then_inc(pv_done, 1)

                    pe.wait_ge(lo_done, 4 * g + 4)
                    pe.wait_ge(v_in[u], 8 * (g - u) + 16)
                    for i in range(2 * NT):
                        half, k = i // NT, i % NT
                        for h in range(2):
                            if i == 0:
                                pe.wait_ge(m_used, mb - 1 + h)
                            bank = t_bank(tb, 2 * i + h)
                            q = slice(half * HALF, (half + 1) * HALF)
                            kk = slice(k * P, (k + 1) * P)
                            pe.matmul(bank[:, :], T1s[u][h][:, kk], T1m[u][h][:, q], start=True, stop=False)
                            pe.matmul(bank[:, :], T2s[u][h][:, kk], T2m[u][h][:, q], start=False, stop=True)\
                                .then_inc(t_ready, 1)
                        if i:
                            values(i - 1)
                        for at, what, args in work:
                            if at == i:
                                what(*args)
                    values(2 * NT - 1)
                    if prep:
                        for h in range(2):
                            max_rows(mb, n0 + M_MAX + h, h, g + 1)

                steps(pe, b, step)
                for n in range(M_SUM):
                    sum_rows(b * M_ALL + M_FIN, n, n, 8 * b + NP - 1, (NP - 1) % 2)

                mc, tc = b * M_ALL + M_C, b * T_ALL + T_C
                pe.wait_ge(norm_done, 8 * b + NP)
                for w in range(M_OUT):
                    bank = m_bank(mc, w)
                    for t in range(2):
                        for f in range(NP):
                            mm = pe.matmul(bank[:, t * D:(t + 1) * D], VS[:, f, (2 * w + t) * P:(2 * w + t + 1) * P],
                                           wo[:, f, :], start=(f == 0), stop=(f == NP - 1))
                    mm.then_inc(m_ready, 1)
                pe.wait_ge(normed, 3 * NT * b + 3 * NT)
                for j in range(T_TR):
                    transposes(t_bank(tc, j), j, n2buf)
                for j in range(M_LORA):
                    k, g = j // 2, j % 2
                    pe.wait_ge(spread_done, KD * b + k + 1)
                    pe.matmul(m_bank(mc, M_OUT + j)[:, :], ones[:, :], D_sb[:, k, LORA * g:LORA * (g + 1), :],
                              start=True, stop=True).then_inc(m_ready, 1)
                pe.wait_ge(m_used, mc + M_OUT + M_LORA)
                for j in range(2 * NH):
                    half, f = j // NH, j % NH
                    bank = t_bank(tc, T_TR + j)
                    for k in range(KD):
                        mm = pe.matmul(bank[:, :], w1_sb[:, k, f * P:(f + 1) * P],
                                       h3T[:, k, half * HALF:(half + 1) * HALF],
                                       start=(k == 0), stop=(k == KD - 1))
                    mm.then_inc(t_ready, 1)
                for w in range(M_FFN2):
                    pe.wait_ge(t_used, tc + T_TR + NH * (w // 2 + 1))
                    bank = m_bank(mc, M_OUT + M_LORA + w)
                    for t in range(2):
                        for f in range(NH):
                            mm = pe.matmul(bank[:, t * D:(t + 1) * D], hid[:, f, (2 * w + t) * P:(2 * w + t + 1) * P],
                                           w2_sb[:, f, :], start=(f == 0), stop=(f == NH - 1))
                    mm.then_inc(m_ready, 1)

        @block.scalar
        def _(act):
            act.wait_ge(const_in, 16 * LOADS)
            act.activation(e_c[:, :], c_sb[:, :], ACT.Exp, scale=-1.0).then_inc(exp_c, 1)

            with act.Fori(0, B) as b:
                def empty(base, j):
                    act.wait_ge(t_ready, base + j + 1)
                    return TB[j % T_RING]

                ta = b * T_ALL
                for j in range(T_TR):
                    k, half = j // NHALF, j % NHALF
                    act.activation(hT[:, k, half * HALF:(half + 1) * HALF], empty(ta, j)[:, :], ACT.Identity,
                                   bias=ln_t[:, KD + k:KD + k + 1], scale=ln_t[:, k:k + 1]).then_inc(t_used, 1)
                for t in range(NT):
                    act.activation(VS[:, NP // 2:NP, t * P:(t + 1) * P],
                                   empty(ta, T_TR + t)[:, :].rearrange("p (f n) -> p f n", n=P),
                                   ACT.Copy).then_inc(t_used, 1)

                def high(n, g, u):
                    if n % 4 == 0:
                        act.wait_ge(rope_done, 4 * g + 2 + 2 * (n // 4))
                    h = n % 2 if n < 4 else n // 2 % 2
                    src = rot[64 * h:64 * h + 64, n // 4, :]
                    if n < 4:
                        dst = T1m[u][h][0:64, :] if n < 2 else T2m[u][h][64:128, :]
                    else:
                        dst = T1s[u][h][0:64, :] if n % 2 == 0 else T1s[u][h][64:128, :]
                    act.activation(dst, src, ACT.Copy).then_inc(hi_done, 1)

                for n in range(8):
                    high(n, 8 * b, 0)

                def output(half, g, p):
                    act.wait_ge(pv_done, PV * g + NT * (half + 1))
                    act.activation(VS[:, bass.ds(p, 1), half * HALF:(half + 1) * HALF],
                                   OB[half][:, :].rearrange("p (a n) -> p a n", a=1), ACT.Copy).then_inc(o_used, 1)

                def step(g, p, u, prep, fin):
                    tb = t_base(b, p)
                    for j in range(T_PAIR):
                        half, k, h = j // (2 * NT), j // 2 % NT, j % 2
                        bank = empty(tb, j)
                        if fin or j >= P_RING:
                            act.wait_ge(pv_done, PV * g + (j - P_RING) // 2 + 1)
                            i = (j - P_RING) // 2
                            ih, ik = i // NT, i % NT
                            act.wait_ge(add_done, ADDS * g + 2 * (NT - 1) * ih + 2 * max(ik - 1, 0) + h + 1)
                        act.activation(Pt[:, j % P_RING, :], bank[:, :], ACT.Exp, scale=SCALE).then_inc(t_used, 1)
                        if fin and j == 3:
                            output(1, g - 1, p - 1)
                        if j == 19:
                            output(0, g, p)
                        if prep and 10 <= j < 18:
                            high(j - 10, g + 1, 1 - u)

                steps(act, b, step)
                output(1, 8 * b + NP - 1, NP - 1)

                tc = b * T_ALL + T_C
                for j in range(T_TR):
                    k, half = j // NHALF, j % NHALF
                    if j == 0:
                        act.wait_ge(cols_done, b + 1)
                    act.activation(h3T[:, k, half * HALF:(half + 1) * HALF], empty(tc, j)[:, :], ACT.Identity,
                                   bias=mod_c[:, k, :], scale=mod_c[:, KD + k, :]).then_inc(t_used, 1)
                for j in range(2 * NH):
                    half, f = j // NH, j % NH
                    act.activation(hid[:, f, half * HALF:(half + 1) * HALF], empty(tc, T_TR + j)[:, :], ACT.Gelu,
                                   bias=b1_t[:, f:f + 1]).then_inc(t_used, 1)

        @block.gpsimd
        def _(pool):
            pool.memset(ones[:, :], 1.0).then_inc(const_set, 1)
            pool.memset(neg_half[:, :], -0.5).then_inc(const_set, 1)
            for u in range(2):
                for h in range(2):
                    pool.memset(T2m[u][h][0:64, :].bitcast(f32), 0.0).then_inc(const_set, 1)
                    pool.memset(T2s[u][h][0:64, :].bitcast(f32), 0.0).then_inc(const_set, 1)
            pool.wait_ge(const_set, 10)
            for u in range(2):
                for h in range(2):
                    pool.memset(T2s[u][h][0:NT, :].bitcast(f32), 1.0).then_inc(const_set, 1)

            with pool.Fori(0, B) as b:
                def inverse_root(n):
                    pool.wait_ge(var_done, 3 * b + n + 1)
                    pool.tensor_tensor(rstd[:, :], ve[:, :], neg_half[:, :], ALU.pow).then_inc(rstd_done, 1)

                inverse_root(0)
                inverse_root(1)

                def step(g, p, u, prep, fin):
                    tb = t_base(b, p)
                    for i in range(2 * NT):
                        half, k = i // NT, i % NT
                        for h in range(2):
                            if k == 0:
                                continue
                            n = 2 * (NT - 1) * half + 2 * (k - 1) + h
                            j = 2 * i + h
                            pool.wait_ge(t_used, tb + j + 1)
                            if k > 1:
                                pool.wait_ge(add_done, ADDS * g + n - 1)
                            sl = acc[:, u, h, half * HALF:(half + 1) * HALF]
                            pool.tensor_tensor(sl, Pt[:, (j - 2) % P_RING, :] if k == 1 else sl,
                                               Pt[:, j % P_RING, :], ALU.add).then_inc(add_done, 1)

                steps(pool, b, step)
                inverse_root(2)

        @block.vector
        def _(dve):
            dve.wait_ge(const_in, 16 * LOADS)
            dve.wait_ge(exp_c, 1)
            dve.tensor_scalar(e_c[:, :], e_c[:, :], 1.0, None, ALU.add).then_inc(setup, 1)
            dve.wait_ge(setup, 1)
            dve.reciprocal(silu_c[:, :], e_c[:, :]).then_inc(setup, 1)
            dve.wait_ge(setup, 2)
            dve.tensor_tensor(silu_c[:, :], silu_c[:, :], c_sb[:, :], ALU.mult).then_inc(silu_done, 1)
            dve.wait_ge(mod_mm, 1)
            for n in range(3):
                dve.tensor_copy(modr[:, n * HALF:(n + 1) * HALF], MB[n][0:B, :]).then_inc(setup, 1)
            dve.tensor_copy(mod_t[:, 0:KD, :],
                            TB[0][:, 0:KD * B].rearrange("p (k b) -> p k b", b=B)).then_inc(setup, 1)
            dve.tensor_scalar(mod_t[:, KD:2 * KD, :],
                              TB[0][:, KD * B:2 * KD * B].rearrange("p (k b) -> p k b", b=B),
                              1.0, None, ALU.add).then_inc(setup, 1)
            dve.wait_ge(setup, 7)
            ca = modr[:, D:2 * D]
            dve.tensor_scalar(ca, ca, 1.0, None, ALU.add).then_inc(rows_done, 1)
            for n, m in enumerate((2, 5)):
                row, sign, size = modr[:, m * D:(m + 1) * D], guard[:, 2 * n, :], guard[:, 2 * n + 1, :]
                dve.tensor_scalar(size, row, -1.0, None, ALU.mult).then_inc(setup, 1)
                dve.tensor_scalar(sign, row, 0.0, 2.0, ALU.is_ge, ALU.mult).then_inc(setup, 1)
                dve.wait_ge(setup, 9 + 4 * n)
                dve.tensor_tensor(size, size, row, ALU.max).then_inc(setup, 1)
                dve.tensor_scalar(sign, sign, -1.0, None, ALU.add).then_inc(setup, 1)
                dve.wait_ge(setup, 11 + 4 * n)
                dve.scalar_tensor_tensor(out=row, in0=size, scalar=0.25, in1=sign, op0=ALU.max,
                                         op1=ALU.mult).then_inc(rows_done, 1)

            with dve.Fori(0, B) as b:
                def layer_norm(n, src, dst):
                    ln = 3 * b + n
                    for t in range(NT):
                        dve.bn_stats(stats[:, t, :], src[:, t, :]).then_inc(stats_done, 1)
                    dve.wait_ge(stats_done, NT * ln + NT)
                    me, qe, mo, qo = (stats[:, :, i] for i in (1, 2, 4, 5))
                    dve.tensor_tensor(mv[:, :, 0], me, mo, ALU.add).then_inc(merged, 1)
                    dve.tensor_tensor(mv[:, :, 1], me, mo, ALU.subtract).then_inc(merged, 1)
                    dve.tensor_tensor(ve[:, :], qe, qo, ALU.add).then_inc(merged, 1)
                    dve.wait_ge(merged, 6 * ln + 3)
                    dve.tensor_scalar(mv[:, :, 0], mv[:, :, 0], 0.5, None, ALU.mult).then_inc(merged, 1)
                    dve.scalar_tensor_tensor(out=mv[:, :, 1], in0=mv[:, :, 1], scalar=0.25, in1=mv[:, :, 1],
                                             op0=ALU.mult, op1=ALU.mult).then_inc(merged, 1)
                    dve.tensor_scalar(ve[:, :], ve[:, :], 1.0 / D, EPS, ALU.mult, ALU.add).then_inc(merged, 1)
                    dve.wait_ge(merged, 6 * ln + 6)
                    dve.tensor_tensor(ve[:, :], ve[:, :], mv[:, :, 1], ALU.add).then_inc(var_done, 1)
                    dve.wait_ge(rstd_done, ln + 1)
                    for t in range(NT):
                        dve.tensor_scalar(dst[:, t, :], src[:, t, :], mv[:, t, 0:1], rstd[:, t:t + 1],
                                          ALU.subtract, ALU.mult).then_inc(normed, 1)

                def row(j, n=NT):
                    return mod_bc[:, j:j + 1, :].broadcast_to([P, n, D])

                dve.wait_ge(x_in, 80 * b + 80)
                layer_norm(0, xt, hbuf)
                dve.wait_ge(normed, 24 * b + 8)
                dve.tensor_tensor(hbuf[:, :, :], hbuf[:, :, :], row(1), ALU.mult).then_inc(modulated, 1)
                dve.wait_ge(modulated, 4 * b + 1)
                dve.tensor_tensor(hbuf[:, :, :], hbuf[:, :, :], row(0), ALU.add).then_inc(modulated, 1)
                dve.wait_ge(modulated, 4 * b + 2)
                layer_norm(1, hbuf, nbuf)
                dve.wait_ge(normed, 24 * b + 16)
                dve.tensor_tensor(hbuf[:, :, :], hbuf[:, :, :], row(2), ALU.mult).then_inc(modulated, 1)
                dve.wait_ge(modulated, 4 * b + 3)
                dve.tensor_tensor(xres[:, :, :], xt[:, :, :], hbuf[:, :, :], ALU.add).then_inc(modulated, 1)

                def filled(base, j):
                    dve.wait_ge(m_ready, base + j + 1)
                    return MB[j % M_RING]

                ma = b * M_ALL
                for j in range(4):
                    kind, half = j // 2, j % 2
                    dve.tensor_copy(cT[:, kind, half * HALF:(half + 1) * HALF], filled(ma, j)[:, :])\
                        .then_inc(m_used, 1)
                for t in range(NT):
                    dve.tensor_copy(VS[:, 0:NP // 2, t * P:(t + 1) * P],
                                    filled(ma, 4 + t)[:, :].rearrange("p (f n) -> p f n", n=P))\
                        .then_inc(m_used, 1)

                for i in range(2):
                    dve.wait_ge(stored[i], 32 * b + 16)

                def rotate(base, g):
                    for j in range(M_PROJ):
                        kind, half, swap = j // 4, j // 2 % 2, j % 2
                        sl = slice(half * HALF, (half + 1) * HALF)
                        dst = tmp[:, half, :] if swap else rot[:, kind, sl]
                        dve.tensor_tensor(dst, filled(base, j)[:, :], cos_sin[:, swap, sl], ALU.mult)\
                            .then_inc(m_used, 1)
                        if swap:
                            dve.wait_ge(m_used, base + j + 1)
                            dve.tensor_tensor(rot[:, kind, sl], rot[:, kind, sl], tmp[:, half, :], ALU.add)\
                                .then_inc(rope_done, 1)

                def low(n, g, u):
                    h, kind = n % 2, n // 2
                    dve.wait_ge(hi_done, 8 * g + (1, 4, 5, 8)[n])
                    rows = slice(64 * h, 64 * h + 64)
                    high = (T1m[u][0], T2m[u][1], T1s[u][0], T1s[u][1])[n][rows, :]
                    dst = (T1m if kind == 0 else T2s)[u][h][64:128, :]
                    dve.tensor_tensor(dst, rot[rows, kind, :], high.bitcast(f32), ALU.subtract)\
                        .then_inc(lo_done, 1)

                def maxima(base, j, n):
                    dve.tensor_reduce(mxp[:, n // 2, n % 2:n % 2 + 1], filled(base, j)[:, :], AX.X, ALU.max)\
                        .then_inc(m_used, 1)

                def rows_of_maxima(base, j, g, u):
                    dve.wait_ge(m_used, base + j)
                    dve.tensor_reduce(mx[:, :], mxp[:, :, :], AX.X, ALU.max).then_inc(max_done, 1)
                    for h in range(2):
                        bank = filled(base, j + h)
                        dve.tensor_tensor(T2m[u][h][0:NT, :].rearrange("t (a n) -> t a n", n=P),
                                          bank[0:NT, 0:P].rearrange("t (a n) -> t a n", a=1)
                                          .broadcast_to([NT, NT, P]),
                                          diag[:, :].rearrange("t (a n) -> t a n", n=1)
                                          .broadcast_to([NT, NT, P]), ALU.mult).then_inc(m_used, 1)

                def take_sums(base, j):
                    for half in range(NHALF):
                        dve.tensor_copy(sums[:, half * HALF:(half + 1) * HALF], filled(base, j + half)[:, :])\
                            .then_inc(m_used, 1)

                def invert(g):
                    dve.wait_ge(cs_in, 32 * g)
                    dve.reciprocal(rc[:, :, :], cs[:, :, :]).then_inc(inv_done, 1)

                def normalise(g, p):
                    dve.wait_ge(rb_in, 32 * g)
                    dve.wait_ge(o_used, 2 * g)
                    sl = VS[:, bass.ds(p, 1), :]
                    dve.tensor_tensor(sl, sl, rb[:, :].rearrange("p (a n) -> p a n", a=1), ALU.mult)\
                        .then_inc(norm_done, 1)

                base = ma + M_PREP0
                rotate(base, 8 * b)
                for n in range(4):
                    low(n, 8 * b, 0)
                for n in range(M_MAX):
                    maxima(base, M_PROJ + n, n)
                rows_of_maxima(base, M_PROJ + M_MAX, 8 * b, 0)

                def step(g, p, u, prep, fin):
                    mb = m_base(b, p)
                    j = 0
                    if prep:
                        rotate(mb, g + 1)
                        j += M_PROJ
                    if fin:
                        take_sums(mb, j)
                        j += M_SUM
                    if prep:
                        for n in range(4):
                            low(n, g + 1, 1 - u)
                        for n in range(M_MAX):
                            maxima(mb, j + n, n)
                            if fin and n == 7:
                                invert(g)
                            if fin and n == 23:
                                normalise(g, p - 1)
                        rows_of_maxima(mb, j + M_MAX, g + 1, 1 - u)
                    elif fin:
                        invert(g)
                        normalise(g, p - 1)

                steps(dve, b, step)
                take_sums(ma + M_FIN, 0)
                invert(8 * b + NP)
                normalise(8 * b + NP, NP - 1)

                mc, tc = ma + M_C, b * T_ALL + T_C
                dve.tensor_copy(mod_c[:, :, :], mod_t[:, :, bass.ds(b, 1)]).then_inc(cols_done, 1)
                for w in range(M_OUT):
                    bank = filled(mc, w)
                    dve.tensor_tensor(obuf[:, w % 2, :, :], bank[:, :].rearrange("p (t d) -> p t d", d=D),
                                      row(2, 2), ALU.mult).then_inc(m_used, 1)
                    dve.wait_ge(m_used, mc + w + 1)
                    sl = xres[:, 2 * w:2 * w + 2, :]
                    dve.tensor_tensor(sl, sl, obuf[:, w % 2, :, :], ALU.add).then_inc(x1_done, 1)
                dve.wait_ge(x1_done, M_OUT * b + M_OUT)
                layer_norm(2, xres, n2buf)
                dve.wait_ge(t_used, tc + T_TR)
                dve.tensor_scalar(sodd[:, :, :], h3T[:, :, 2:2 + 4 * LORA:2], ls_bc[:, 0:1], None, ALU.mult)\
                    .then_inc(odd_done, 1)
                for k in range(KD):
                    dve.tensor_tensor(D_sb[:, k, :, :],
                                      ident[:, :].rearrange("p (a n) -> p a n", a=1)
                                      .broadcast_to([P, 2 * LORA, P]),
                                      h3T[:, k, 1:1 + 4 * LORA:2].rearrange("p (a n) -> p a n", n=1)
                                      .broadcast_to([P, 2 * LORA, P]), ALU.mult).then_inc(spread_done, 1)
                dve.wait_ge(odd_done, b + 1)
                dve.wait_ge(wc_in, 32 * b + 32)
                for j in range(M_LORA):
                    k, second = j // 2, j % 2
                    bank = filled(mc, M_OUT + j)
                    for i in range(LORA):
                        even = bank[:, i * P:(i + 1) * P]
                        for s in range(KD):
                            if second:
                                dst = w2_sb[:, s:NH:KD, 64 * i + 32 * k:64 * i + 32 * k + 32]
                                src = even.rearrange("p (a c) -> p c a", c=4)
                            else:
                                dst = w1_sb[:, s, D * i + P * k:D * i + P * (k + 1)]
                                src = even
                            last = dve.scalar_tensor_tensor(
                                out=dst, in0=src, scalar=sodd[:, s, LORA * second + i:LORA * second + i + 1],
                                in1=dst, op0=ALU.mult, op1=ALU.add)
                    last.then_inc(m_used, 1)
                for w in range(M_FFN2):
                    if w >= 2:
                        dve.wait_ge(stored[w % 2], 16 + 32 * b + 16 * (w // 2))
                    bank = filled(mc, M_OUT + M_LORA + w)
                    o = obuf[:, w % 2, :, :]
                    dve.tensor_tensor(o, bank[:, :].rearrange("p (t d) -> p t d", d=D),
                                      b2_bc[:, :].rearrange("p (a d) -> p a d", a=1).broadcast_to([P, 2, D]),
                                      ALU.add).then_inc(m_used, 1)
                    dve.wait_ge(m_used, mc + M_OUT + M_LORA + w + 1)
                    dve.tensor_tensor(o, o, row(3, 2), ALU.mult).then_inc(gated, 1)
                    dve.wait_ge(gated, M_FFN2 * b + w + 1)
                    dve.tensor_tensor(o, o, xres[:, 2 * w:2 * w + 2, :], ALU.add).then_inc(out_ready, 1)


def kernel(**inputs):
    import numpy as np
    import concourse.bacc as bacc
    from concourse.bass_utils import run_bass_kernel_spmd

    a = {n.removeprefix("L0_"): np.asarray(v) for n, v in inputs.items()}

    inv_freq = 1.0 / 10000.0 ** (np.arange(0, DH, 2, dtype=np.float32) / DH)
    freqs = np.outer(np.arange(S, dtype=np.float32), inv_freq)
    cos = np.concatenate([np.cos(freqs), np.cos(freqs)], -1)[:, ::2].T
    sin = np.concatenate([np.sin(freqs), np.sin(freqs)], -1)[:, ::2].T
    signed = np.stack([-sin, sin], 1)
    rope = np.stack([np.tile(np.repeat(cos, 2, 0), (2, 1)),
                     np.tile(signed.reshape(DH, S), (2, 1))], 1).astype(np.float32)

    def pairs(w):
        return w.reshape(NP, P, R).transpose(0, 2, 1)

    def swapped(w):
        return w.reshape(-1, 2, R)[:, ::-1, :].reshape(w.shape)

    def tiles(w):
        return w.reshape(-1, P, w.shape[1]).transpose(1, 0, 2)

    wq, wk = a["attn_w_up_q"], a["attn_w_up_k"]
    arrays = {
        "x": a["attn_x"],
        "w_pair": np.stack([pairs(wq), pairs(swapped(wq)), pairs(wk), pairs(swapped(wk))], 2),
        "w_v": a["attn_w_up_v"].T,
        "w_down": np.stack([tiles(a["attn_w_down_q"].T), tiles(a["attn_w_down_kv"].T)], 2),
        "w_out": tiles(a["attn_w_out"].T),
        "w1": tiles(a["ffn_W1"].T),
        "w2": tiles(a["ffn_W2"].T),
        "ln_cols": np.concatenate([a["attn_ln_scale"].reshape(KD, P), a["attn_ln_bias"].reshape(KD, P)]).T,
        "b1_cols": a["ffn_b1"].reshape(NH, P).T,
        "b2": a["ffn_b2"].reshape(1, D),
        "lora_scale": a["ffn_scale"].reshape(1, 1),
        "c_cols": tiles(a["c"].T).reshape(P, KD * B),
        "w_mod": tiles(a["wmod"]),
        "rope": rope,
        "ident_in": np.eye(P, dtype=np.float32),
        "diag_in": -np.eye(NT, dtype=np.float32),
    }
    nc = bacc.Bacc("TRN2", target_bir_lowering=False, num_devices=1)
    args, sent = {}, {}
    for name, v in arrays.items():
        v = np.ascontiguousarray(v)
        sent[f"in_{name}"] = v
        args[name] = nc.dram_tensor(f"in_{name}", v.shape, mybir.dt.from_np(v.dtype), kind="ExternalInput").ap()
    args["out"] = nc.dram_tensor("out_0", (B, S, D), mybir.dt.float32, kind="ExternalOutput").ap()
    build(nc, **args)
    return run_bass_kernel_spmd(nc, [sent], core_ids=[0]).results[0]["out_0"]
```

```python
from contextlib import ExitStack

import concourse.bass as bass
from concourse import mybir

B, S, D = 8, 1024, 256
H, DH = 16, 64
R = 128
HID = 1024
P = 128
NP = H // 2
NT = S // P
KD = D // P
NH = HID // P
HALF = 512
NHALF = S // HALF
TPH = HALF // P
LORA = 4
EPS = 1e-5
SCALE = DH ** -0.5

M_RING = 3
M_PROJ, M_SUM, M_MAX, M_ROW = 8, 2, 4 * NT, 2


def step_units(prep, fin):
    units = []
    if prep:
        units += [(n, "proj", n) for n in range(M_PROJ)]
    if fin:
        units += [(n * 12 // 16, "max2", n) for n in range(M_MAX // 2)]
        units += [(13, "rows2", 0)] + [(12 + n, "sum", n) for n in range(M_SUM)]
    if prep:
        units += [(16 + n * 12 // 16, "max1", n) for n in range(M_MAX // 2)]
        units += [(30, "rows1", 0)]
    return sorted(units, key=lambda unit: unit[0])


M_FIRST, M_STEP = len(step_units(True, False)), len(step_units(True, True))
M_BEFORE = M_PROJ + M_MAX + M_ROW
M_LAST = M_FIRST + (NP - 2) * M_STEP
M_FIN = M_LAST + len(step_units(False, True))
M_OUT = M_FIN + M_SUM
M_PROJ0 = M_OUT + NT // 2
M_LORA = M_PROJ0 + M_PROJ
M_TAIL = M_LORA + 4
QUARTERS = NT // 2
M_ALL = M_TAIL + M_MAX + M_ROW + QUARTERS
T_RING = 3
T_TR, T_C, T_V = 4, 4, 2 * NT
T_A = T_TR + T_C + T_V
T_PAIR = 4 * NT
T_NEXT = NP * T_PAIR
T_TR2 = T_NEXT + T_A
T_FFN = T_TR2 + T_TR
T_ALL = T_FFN + QUARTERS * NH // 2
TAIL = [("ffn1", 0), ("max", 0, 6), ("ffn1", 1), ("max", 6, 12), ("ffn2", 0), ("max", 12, 18),
        ("ffn1", 2), ("max", 18, 24), ("ffn2", 1), ("max", 24, 28), ("ffn1", 3), ("max", 28, 32),
        ("rows",), ("ffn2", 2), ("ffn2", 3)]
FFN2_AT = []
for _what, *_n in TAIL:
    if _what == "ffn2":
        _done = TAIL[:TAIL.index((_what, *_n))]
        FFN2_AT.append(sum({"max": lambda a, z: z - a, "rows": lambda: 2, "ffn2": lambda q: 1,
                            "ffn1": lambda q: 0}[w](*m) for w, *m in _done))
P_RING = 8
ADDS = 4 * (NT - 1)
PV = 2 * NT


LOWS_AT = 13
HIGH_AT = (5, 6, 7, 8, 10, 11, 12, 13)


def b_given(n):
    return not (isinstance(n, int) and n == 0)


def build(nc, x, w_pair, w_v, w_down, w_out, w1, w2, ln_cols, b1_cols, b2, lora_scale,
          c_cols, w_mod, rope, ident_in, diag_in, out):
    f32, f32r = mybir.dt.float32, mybir.dt.float32r
    ALU, ACT, AX = mybir.AluOpType, mybir.ActivationFunctionType, mybir.AxisListType

    mod_d = nc.dram_tensor("mod_rows", [B, 6 * D], f32, kind="Internal").ap()
    base_d = nc.dram_tensor("first_base", [P, NT, D], f32, kind="Internal").ap()
    inv_d = nc.dram_tensor("inverse_sums", [2, S], f32, kind="Internal").ap()

    ctx = ExitStack()
    with ctx:
        def sb(name, shape, dt=f32, stack=ctx):
            return stack.enter_context(nc.sbuf_tensor(name, shape, dt))

        def sem(name):
            return ctx.enter_context(nc.semaphore(name))

        ident = sb("ident", [P, P])
        ones = sb("ones", [P, P])
        diag = sb("diag", [NT, NT])
        neg_half = sb("neg_half", [P, NT])
        ln_t = sb("ln_t", [P, 2 * KD])
        b1_t = sb("b1_t", [P, NH])
        b2_bc = sb("b2_bc", [P, D])
        ls_bc = sb("ls_bc", [P, 1])
        mod_t = sb("mod_t", [P, 2 * KD, B])
        mod_c = sb("mod_c", [P, 2 * KD, 1])
        cos_sin = sb("cos_sin", [P, 2, S])
        wo = sb("wo", [P, NP, D])
        mod_a = sb("mod_a", [P, 3, D])
        mod_b = sb("mod_b", [P, 2, D])
        wd = sb("wd", [P, KD, 2, R])
        xres = sb("xres", [P, NT, D])
        cT = sb("cT", [P, 2, S])
        VS = sb("VS", [P, NP, S])
        wp = [sb(f"wp{u}", [P, 4, P]) for u in range(2)]
        sums = sb("sums", [P, S])
        rb = sb("rb", [P, S])
        cs = sb("cs", [P, 2, NT])
        rc = sb("rc", [P, 2, NT])
        stats = sb("stats", [P, NT, 6])
        mv = sb("mv", [P, NT, 2])
        ve = sb("ve", [P, NT])
        rstd = sb("rstd", [P, NT])
        mxp = sb("mxp", [P, NHALF, NT, 2])
        mx = sb("mx", [P, NHALF, NT])
        sodd = sb("sodd", [P, KD, 2 * LORA])
        T2m = [[sb(f"T2m{u}{h}", [P, S], f32r) for h in range(2)] for u in range(2)]
        T2s = [[sb(f"T2s{u}{h}", [P, S], f32r) for h in range(2)] for u in range(2)]

        def shared(*layouts):
            made = []
            for n, layout in enumerate(layouts):
                stack = ctx if n == len(layouts) - 1 else ExitStack()
                made += [sb(name, shape, dt, stack) for name, shape, dt in layout]
                if n < len(layouts) - 1:
                    stack.close()
            return made

        xt, hbuf, _, hT, *t1 = shared(
            [("xt", [P, NT, D], f32), ("hbuf", [P, NT, D], f32)],
            [("below_hT", [P, NT, D], f32), ("hT", [P, KD, S], f32)],
            [(f"T1{k}0{h}", [P, S], f32r) for k in "ms" for h in range(2)])
        hid, *t2 = shared([("hid", [P, 2, NH, 2 * P], f32)],
                          [(f"T1{k}1{h}", [P, S], f32r) for k in "ms" for h in range(2)])
        T1m, T1s = [t1[0:2], t2[0:2]], [t1[2:4], t2[2:4]]
        w1_sb, w2_sb, Pt = shared(
            [("w1_sb", [P, KD, HID], f32), ("w2_sb", [P, NH, D], f32)],
            [("Pt", [P, P_RING, HALF], f32)])
        n2buf, D_sb, acc = shared(
            [("n2buf", [P, NT, D], f32), ("D_sb", [P, KD, 2 * LORA, P], f32)],
            [("acc", [P, 2, 2, S], f32)])
        wv, h3T, Vp0, Vp1 = shared([("wv", [P, H * DH], f32)], [("h3T", [P, KD, S], f32)],
                                   [("Vp0", [P, NT, P], f32), ("Vp1", [P, NT, P], f32)])
        Vp = [Vp0, Vp1]
        nbuf, rot = shared([("nbuf", [P, NT, D], f32)], [("rot", [P, 2, S], f32)])
        obuf, tmp = shared([("obuf", [P, 2, 2, D], f32)], [("tmp", [P, 2, HALF], f32)])
        c_sb, e_c, silu_c = (sb(n, [P, KD * B]) for n in ("c_sb", "e_c", "silu_c"))
        wm = VS[:, 0:3, :].rearrange("p a s -> p (a s)").rearrange("p (k n) -> p k n", k=KD)
        modr = VS[0:B, 3:5, :].rearrange("p a s -> p (a s)")[:, 0:6 * D]
        guard = VS[0:B, 5, :].rearrange("p (k d) -> p k d", d=D)

        MB = [ctx.enter_context(nc.psum_tensor(f"M{i}", [P, HALF], f32)) for i in range(M_RING)]
        TB = [ctx.enter_context(nc.psum_tensor(f"T{i}", [P, HALF], f32)) for i in range(T_RING)]
        OB = [ctx.enter_context(nc.psum_tensor(f"O{i}", [P, HALF], f32)) for i in range(2)]

        const_in = sem("const_in")
        const_set = sem("const_set")
        setup = sem("setup")
        exp_c, silu_done = sem("exp_c"), sem("silu_done")
        mod_mm = sem("mod_mm")
        rows_done = sem("rows_done")
        m_ready = sem("m_ready")
        m_used = sem("m_used")
        t_ready = sem("t_ready")
        t_used = sem("t_used")
        rope_done = sem("rope_done")
        hi_done = sem("hi_done")
        lo_done = sem("lo_done")
        max_done = sem("max_done")
        pv_done = sem("pv_done")
        add_done = sem("add_done")
        o_used = sem("o_used")
        inv_done = sem("inv_done")
        norm_done = sem("norm_done")
        x_in = sem("x_in")
        wv_in = sem("wv_in")
        base_out, base_in = sem("base_out"), sem("base_in")
        wc_in = sem("wc_in")
        wp_in = [sem(f"wp_in{u}") for u in range(2)]
        v_in = [sem(f"v_in{u}") for u in range(2)]
        cs_in, inv_out, rb_in = sem("cs_in"), sem("inv_out"), sem("rb_in")
        stats_done, merged, var_done = sem("stats_done"), sem("merged"), sem("var_done")
        rstd_done = sem("rstd_done")
        normed = sem("normed")
        modulated = sem("modulated")
        cols_done = sem("cols_done")
        x1_done = sem("x1_done")
        odd_done, spread_done = sem("odd_done"), sem("spread_done")
        gated = sem("gated")
        out_ready = sem("out_ready")
        stored = [sem(f"stored{i}") for i in range(2)]

        LOADS = 11

        block = ctx.enter_context(nc.Block())

        def steps(eng, b, step):
            step(8 * b, 0, 0, True, False)
            with eng.Fori(0, (NP - 2) // 2) as i:
                for r in (1, 2):
                    step(8 * b + (2 * i + r), 2 * i + r, r % 2, True, True)
            step(8 * b + NP - 1, NP - 1, (NP - 1) % 2, False, True)

        def m_at(b, offset):
            return M_BEFORE + b * M_ALL + offset

        def m_base(b, p):
            if isinstance(p, int) and p == 0:
                return m_at(b, 0)
            return m_at(b, M_FIRST + (p - 1) * M_STEP)

        def last_sum(prep):
            return 1 + max(n for n, (_, what, _) in enumerate(step_units(prep, True)) if what == "sum")

        def t_at(b, offset):
            return T_A + b * T_ALL + offset

        @block.sync
        def _(sp):
            for dst, src in ((ident[:, :], ident_in), (diag[:, :], diag_in), (ln_t[:, :], ln_cols),
                             (b1_t[:, :], b1_cols), (b2_bc[:, :], b2.partition_broadcast(P)),
                             (ls_bc[:, :], lora_scale.partition_broadcast(P)),
                             (c_sb[:, :], c_cols), (wm, w_mod),
                             (cos_sin[:, :, :], rope), (wo[:, :, :], w_out), (wd[:, :, :, :], w_down)):
                sp.dma_start(dst, src).then_inc(const_in, 16)
            sp.wait_ge(rows_done, 3)
            for i in range(2):
                half = slice(i * B // 2, (i + 1) * B // 2)
                sp.dma_start(mod_d[half, :], modr[half, :]).then_inc(stored[i], 16)
            for i in range(2):
                sp.wait_ge(stored[i], 16)

            def finish(g, m_sums):
                sp.wait_ge(m_used, m_sums)
                for h in range(2):
                    sp.dma_start(cs[:, h, :], sums[64 * h:64 * h + 1, :]).then_inc(cs_in, 16)
                sp.wait_ge(inv_done, g)
                for h in range(2):
                    sp.dma_start(inv_d[h, :].rearrange("(p j) -> p j", p=P), rc[:, h, :]).then_inc(inv_out, 16)
                sp.wait_ge(inv_out, 32 * g)
                for h in range(2):
                    sp.dma_start(rb[64 * h:64 * h + 64, :], inv_d[h:h + 1, :].partition_broadcast(64))\
                        .then_inc(rb_in, 16)

            def load_a(b):
                sp.dma_start(xt[:, :, :], x[bass.ds(b, 1), :, :].rearrange("a (t p) d -> p (a t) d", p=P))\
                    .then_inc(x_in, 16)
                for m in range(3):
                    sp.dma_start(mod_a[:, m:m + 1, :],
                                 mod_d[bass.ds(b, 1), m * D:(m + 1) * D].partition_broadcast(P))\
                        .then_inc(x_in, 16)
                sp.dma_start(wv[:, :], w_v).then_inc(wv_in, 16)
                sp.dma_start(wp[0][:, :, :], w_pair[0]).then_inc(wp_in[0], 16)

            def load_b(b):
                sp.dma_start(xres[:, :, :], base_d).then_inc(base_in, 16)
                for j, m in enumerate((2, 5)):
                    sp.dma_start(mod_b[:, j:j + 1, :],
                                 mod_d[bass.ds(b, 1), m * D:(m + 1) * D].partition_broadcast(P))\
                        .then_inc(base_in, 16)

            load_a(0)
            sp.wait_ge(modulated, 4)
            sp.dma_start(base_d, xt[:, :, :]).then_inc(base_out, 16)
            sp.wait_ge(base_out, 16)
            load_b(0)
            sp.wait_ge(t_used, T_A)
            sp.dma_start(Vp[0][:, :, :], VS[:, 0, :]).then_inc(v_in[0], 16)

            with sp.Fori(0, B) as b:
                after = (b + 1) % B

                def step(g, p, u, prep, fin):
                    if prep:
                        if fin:
                            sp.wait_ge(pv_done, PV * g - PV + 1)
                        sp.dma_start(wp[1 - u][:, :, :], w_pair[bass.ds(p + 1, 1), :, :, :]
                                     .rearrange("a p k n -> p (a k) n")).then_inc(wp_in[1 - u], 16)
                        if fin:
                            sp.wait_ge(pv_done, PV * g)
                        sp.dma_start(Vp[1 - u][:, :, :], VS[:, bass.ds(p + 1, 1), :]).then_inc(v_in[1 - u], 16)
                    else:
                        sp.wait_ge(pv_done, PV * g)
                        load_a(after)
                    if fin:
                        finish(g, m_base(b, p) + last_sum(prep))

                steps(sp, b, step)
                sp.wait_ge(modulated, 4 * b + 8)
                sp.dma_start(base_d, xt[:, :, :]).then_inc(base_out, 16)
                sp.wait_ge(pv_done, PV * 8 * b + PV * NP)
                sp.wait_ge(add_done, ADDS * 8 * b + ADDS * NP)
                sp.dma_start(w1_sb[:, :, :], w1).then_inc(wc_in, 16)
                sp.dma_start(w2_sb[:, :, :], w2).then_inc(wc_in, 16)
                finish(8 * b + NP, m_at(b, M_OUT))
                for w in range(QUARTERS):
                    if w == 2:
                        sp.wait_ge(t_used, t_at(b, T_ALL))
                        sp.dma_start(Vp[0][:, :, :], VS[:, 0, :]).then_inc(v_in[0], 16)
                    sp.wait_ge(out_ready, 4 * b + w + 1)
                    sp.dma_start(out[bass.ds(b, 1), 2 * w * P:2 * (w + 1) * P, :]
                                 .rearrange("a (t p) d -> p (a t) d", p=P), obuf[:, w % 2, :, :])\
                        .then_inc(stored[w % 2], 16)
                sp.wait_ge(base_out, 16 * b + 32)
                load_b(after)
            for i in range(2):
                sp.wait_ge(stored[i], 16 + 32 * B)
            sp.wait_ge(base_in, 48 * (B + 1))
            sp.wait_ge(v_in[0], 16 * (4 * B + 1))

        @block.tensor
        def _(pe):
            pe.wait_ge(const_in, 16 * LOADS)
            pe.wait_ge(silu_done, 1)
            for n in range(3):
                for k in range(KD):
                    mm = pe.matmul(MB[n][0:B, :], silu_c[:, k * B:(k + 1) * B],
                                   wm[:, k, n * HALF:(n + 1) * HALF], start=(k == 0), stop=(k == KD - 1))
            for j in range(2 * KD):
                for k in range(KD):
                    mm = pe.matmul(TB[0][:, j * B:(j + 1) * B], wm[:, k, 3 * D + j * P:3 * D + (j + 1) * P],
                                   silu_c[:, k * B:(k + 1) * B], start=(k == 0), stop=(k == KD - 1))
            mm.then_inc(mod_mm, 1)
            pe.wait_ge(const_set, 14)
            pe.wait_ge(rows_done, 3)

            def m_bank(base, j):
                pe.wait_ge(m_used, base if j < M_RING else base + (j - M_RING + 1))
                return MB[j % M_RING]

            def t_bank(base, j):
                if j >= T_RING:
                    pe.wait_ge(t_used, base + (j - T_RING + 1))
                elif not (isinstance(base, int) and base == 0):
                    pe.wait_ge(t_used, base)
                return TB[j % T_RING]

            def transposes(base, j, src):
                k, half = j // NHALF, j % NHALF
                bank = t_bank(base, j)
                for c in range(TPH):
                    mm = pe.transpose(bank[:, c * P:(c + 1) * P],
                                      src[:, TPH * half + c, k * P:(k + 1) * P], ident[:, :])
                mm.then_inc(t_ready, 1)

            def low_rank(base):
                for j in range(T_TR):
                    transposes(base, j, nbuf)
                pe.wait_ge(t_used, base + T_TR)
                for j in range(T_C):
                    kind, half = j // 2, j % 2
                    bank = t_bank(base + T_TR, j)
                    for k in range(KD):
                        mm = pe.matmul(bank[:, :], wd[:, k, kind, :], hT[:, k, half * HALF:(half + 1) * HALF],
                                       start=(k == 0), stop=(k == KD - 1))
                    mm.then_inc(t_ready, 1)

            def v_of(base):
                pe.wait_ge(t_used, base)
                for j in range(T_V):
                    t, f = j // 2, j % 2
                    pe.matmul(t_bank(base, j)[:, :], cT[:, 1, t * P:(t + 1) * P], wv[:, f * HALF:(f + 1) * HALF],
                              start=True, stop=True).then_inc(t_ready, 1)

            def proj(base, j, n, g, u):
                if n == 0:
                    pe.wait_ge(wp_in[u], 8 * (g - u) + 16)
                kind, half, swap = n // 4, n // 2 % 2, n % 2
                pe.matmul(m_bank(base, j)[:, :], wp[u][:, 2 * kind + swap, :],
                          cT[:, kind, half * HALF:(half + 1) * HALF],
                          start=True, stop=True).then_inc(m_ready, 1)

            def scores_max(base, j, n, g, u):
                if n == 0:
                    pe.wait_ge(hi_done, 8 * g + 8)
                    pe.wait_ge(lo_done, 4 * g + 2)
                part, h, t, half = n // (2 * NT), n // NT % 2, n // 2 % TPH, n % 2
                t += TPH * part
                pe.matmul(m_bank(base, j)[:, :], T1m[u][h][:, t * P:(t + 1) * P],
                          T1s[u][h][:, half * HALF:(half + 1) * HALF],
                          start=True, stop=True).then_inc(m_ready, 1)

            def max_rows(base, j, part, g):
                pe.wait_ge(max_done, 2 * g + part + 1)
                pe.transpose(m_bank(base, j)[0:NT, 0:P], mx[:, part, :], ident[:, :])\
                    .then_inc(m_ready, 1)

            def sum_rows(base, j, half, g, u):
                pe.wait_ge(add_done, ADDS * g + ADDS)
                bank = m_bank(base, j)
                for h in range(2):
                    mm = pe.matmul(bank[64 * h:64 * h + 64, :], ones[:, 0:64],
                                   acc[:, u, h, half * HALF:(half + 1) * HALF], start=True, stop=True)
                mm.then_inc(m_ready, 1)

            pe.wait_ge(modulated, 4)
            low_rank(0)
            pe.wait_ge(wv_in, 16)
            v_of(T_TR + T_C)
            for j in range(M_PROJ):
                proj(0, j, j, 0, 0)
            for n in range(M_MAX):
                scores_max(0, M_PROJ + n, n, 0, 0)
            for h in range(2):
                max_rows(0, M_PROJ + M_MAX + h, h, 0)

            with pe.Fori(0, B) as b:
                def step(g, p, u, prep, fin):
                    mb, tb = m_base(b, p), t_at(b, p * T_PAIR)
                    units = step_units(prep, fin)
                    rows2 = [what for _, what, _ in units].index("rows2") if fin else 0

                    def work(j, what, n):
                        if what == "proj":
                            proj(mb, j, n, g + 1, 1 - u)
                        elif what == "sum":
                            sum_rows(mb, j, n, g - 1, 1 - u)
                        elif what == "max1":
                            scores_max(mb, j, n, g + 1, 1 - u)
                        elif what == "max2":
                            scores_max(mb, j, M_MAX // 2 + n, g, u)
                        elif what == "rows1":
                            max_rows(mb, j, 0, g + 1)
                        else:
                            max_rows(mb, j, 1, g)

                    def values(i):
                        half, k = i // NT, i % NT
                        pe.wait_ge(t_used, tb + 2 * i + 2)
                        if k == 0 and fin:
                            pe.wait_ge(o_used, 2 * g - 1 + half)
                        if i == 0:
                            pe.wait_ge(v_in[u], 8 * (g - u) + 16)
                        for h in range(2):
                            mm = pe.matmul(OB[half][64 * h:64 * h + 64, :], Vp[u][:, k, 64 * h:64 * h + 64],
                                           Pt[:, (2 * i + h) % P_RING, :], start=(k == 0), stop=(k == NT - 1))
                        mm.then_inc(pv_done, 1)

                    pe.wait_ge(lo_done, 4 * g + 4)
                    for i in range(2 * NT):
                        half, k = i // NT, i % NT
                        if i == 0:
                            pe.wait_ge(m_used, mb)
                        if i == NT and fin:
                            pe.wait_ge(m_used, mb + rows2 + 1)
                        for h in range(2):
                            bank = t_bank(tb, 2 * i + h)
                            q = slice(half * HALF, (half + 1) * HALF)
                            kk = slice(k * P, (k + 1) * P)
                            pe.matmul(bank[:, :], T1s[u][h][:, kk], T1m[u][h][:, q], start=True, stop=False)
                            pe.matmul(bank[:, :], T2s[u][h][:, kk], T2m[u][h][:, q], start=False, stop=True)\
                                .then_inc(t_ready, 1)
                        for slot in range(2):
                            if slot and i:
                                values(i - 1)
                            for j, (at, what, n) in enumerate(units):
                                if at == 2 * i + slot:
                                    work(j, what, n)
                    values(2 * NT - 1)

                steps(pe, b, step)

                pe.wait_ge(modulated, 4 * b + 8)
                low_rank(t_at(b, T_NEXT))
                for n in range(M_SUM):
                    sum_rows(m_at(b, M_FIN), n, n, 8 * b + NP - 1, (NP - 1) % 2)

                pe.wait_ge(norm_done, 8 * b + NP)
                for w in range(NT // 2):
                    bank = m_bank(m_at(b, M_OUT), w)
                    for t in range(2):
                        for f in range(NP):
                            mm = pe.matmul(bank[:, t * D:(t + 1) * D], VS[:, f, (2 * w + t) * P:(2 * w + t + 1) * P],
                                           wo[:, f, :], start=(f == 0), stop=(f == NP - 1))
                    mm.then_inc(m_ready, 1)

                pe.wait_ge(wv_in, 16 * b + 32)
                v_of(t_at(b, T_NEXT + T_TR + T_C))
                for j in range(M_PROJ):
                    proj(m_at(b, M_PROJ0), j, j, 8 * b + 8, 0)

                pe.wait_ge(normed, 3 * NT * b + 5 * NT)
                for j in range(T_TR):
                    transposes(t_at(b, T_TR2), j, n2buf)
                for j in range(4):
                    g, k = j // 2, j % 2
                    pe.wait_ge(spread_done, KD * b + k + 1)
                    pe.matmul(m_bank(m_at(b, M_LORA), j)[:, :], ones[:, :], D_sb[:, k, LORA * g:LORA * (g + 1), :],
                              start=True, stop=True).then_inc(m_ready, 1)
                mt, j = m_at(b, M_TAIL), 0
                for what, *n in TAIL:
                    if what == "ffn1":
                        q, = n
                        pe.wait_ge(m_used, m_at(b, M_LORA + 2))
                        for f in range(0, NH, 2):
                            bank = t_bank(t_at(b, T_FFN), q * NH // 2 + f // 2)
                            for s in range(2):
                                for k in range(KD):
                                    mm = pe.matmul(bank[:, s * 2 * P:(s + 1) * 2 * P],
                                                   w1_sb[:, k, (f + s) * P:(f + s + 1) * P],
                                                   h3T[:, k, q * 2 * P:(q + 1) * 2 * P],
                                                   start=(k == 0), stop=(k == KD - 1))
                            mm.then_inc(t_ready, 1)
                    elif what == "ffn2":
                        q, = n
                        pe.wait_ge(m_used, m_at(b, M_TAIL))
                        pe.wait_ge(t_used, t_at(b, T_FFN + (q + 1) * NH // 2))
                        bank = m_bank(mt, j)
                        for t in range(2):
                            for f in range(NH):
                                mm = pe.matmul(bank[:, t * D:(t + 1) * D], hid[:, q % 2, f, t * P:(t + 1) * P],
                                               w2_sb[:, f, :], start=(f == 0), stop=(f == NH - 1))
                        mm.then_inc(m_ready, 1)
                        j += 1
                    elif what == "max":
                        for m in range(*n):
                            scores_max(mt, j, m, 8 * b + 8, 0)
                            j += 1
                    else:
                        for h in range(2):
                            max_rows(mt, j, h, 8 * b + 8)
                            j += 1

        @block.scalar
        def _(act):
            act.wait_ge(const_in, 16 * LOADS)
            act.activation(e_c[:, :], c_sb[:, :], ACT.Exp, scale=-1.0).then_inc(exp_c, 1)

            def empty(base, j):
                act.wait_ge(t_ready, base + j + 1)
                return TB[j % T_RING]

            def take_low_rank(base):
                for j in range(T_TR):
                    k, half = j // NHALF, j % NHALF
                    act.activation(hT[:, k, half * HALF:(half + 1) * HALF], empty(base, j)[:, :], ACT.Identity,
                                   bias=ln_t[:, KD + k:KD + k + 1], scale=ln_t[:, k:k + 1]).then_inc(t_used, 1)
                for j in range(T_C):
                    kind, half = j // 2, j % 2
                    act.activation(cT[:, kind, half * HALF:(half + 1) * HALF], empty(base + T_TR, j)[:, :],
                                   ACT.Copy).then_inc(t_used, 1)

            def take_v(base):
                for j in range(T_V):
                    t, f = j // 2, j % 2
                    act.activation(VS[:, f * NP // 2:(f + 1) * NP // 2, t * P:(t + 1) * P],
                                   empty(base, j)[:, :].rearrange("p (f n) -> p f n", n=P),
                                   ACT.Copy).then_inc(t_used, 1)

            def high(n, g, u):
                if n % 4 == 0:
                    act.wait_ge(rope_done, 4 * g + 2 + 2 * (n // 4))
                h = n % 2 if n < 4 else n // 2 % 2
                src = rot[64 * h:64 * h + 64, n // 4, :]
                if n < 4:
                    dst = T1m[u][h][0:64, :] if n < 2 else T2m[u][h][64:128, :]
                else:
                    dst = T1s[u][h][0:64, :] if n % 2 == 0 else T1s[u][h][64:128, :]
                act.activation(dst, src, ACT.Copy).then_inc(hi_done, 1)

            take_low_rank(0)
            take_v(T_TR + T_C)
            act.wait_ge(base_out, 16)
            for n in range(8):
                high(n, 0, 0)

            with act.Fori(0, B) as b:
                def output(half, g, p):
                    act.wait_ge(pv_done, PV * g + NT * (half + 1))
                    act.activation(VS[:, bass.ds(p, 1), half * HALF:(half + 1) * HALF],
                                   OB[half][:, :].rearrange("p (a n) -> p a n", a=1), ACT.Copy).then_inc(o_used, 1)

                def step(g, p, u, prep, fin):
                    tb = t_at(b, p * T_PAIR)
                    for j in range(T_PAIR):
                        half, k, h = j // (2 * NT), j // 2 % NT, j % 2
                        bank = empty(tb, j)
                        if fin or j >= P_RING:
                            act.wait_ge(pv_done, PV * g + (j - P_RING) // 2 + 1)
                            i = (j - P_RING) // 2
                            ih, ik = i // NT, i % NT
                            act.wait_ge(add_done, ADDS * g + 2 * (NT - 1) * ih + 2 * max(ik - 1, 0) + h + 1)
                        act.activation(Pt[:, j % P_RING, :], bank[:, :], ACT.Exp, scale=SCALE).then_inc(t_used, 1)
                        if fin and j == 3:
                            output(1, g - 1, p - 1)
                        if j == 19:
                            output(0, g, p)
                        if prep and j in HIGH_AT:
                            high(HIGH_AT.index(j), g + 1, 1 - u)

                steps(act, b, step)
                output(1, 8 * b + NP - 1, NP - 1)
                take_low_rank(t_at(b, T_NEXT))
                take_v(t_at(b, T_NEXT + T_TR + T_C))

                act.wait_ge(cols_done, b + 1)
                for j in range(T_TR):
                    k, half = j // NHALF, j % NHALF
                    act.activation(h3T[:, k, half * HALF:(half + 1) * HALF], empty(t_at(b, T_TR2), j)[:, :],
                                   ACT.Identity, bias=mod_c[:, k, :], scale=mod_c[:, KD + k, :]).then_inc(t_used, 1)
                act.wait_ge(base_out, 16 * b + 32)
                for n in range(8):
                    high(n, 8 * b + 8, 0)
                for q in range(QUARTERS):
                    for f in range(0, NH, 2):
                        j = q * NH // 2 + f // 2
                        bank = empty(t_at(b, T_FFN), j)
                        if q >= 2:
                            act.wait_ge(m_ready, m_at(b, M_TAIL) + FFN2_AT[q - 2] + 1)
                        act.activation(hid[:, q % 2, f, :], bank[:, 0:2 * P], ACT.Gelu, bias=b1_t[:, f:f + 1])
                        act.activation(hid[:, q % 2, f + 1, :], bank[:, 2 * P:4 * P], ACT.Gelu,
                                       bias=b1_t[:, f + 1:f + 2]).then_inc(t_used, 1)

        @block.gpsimd
        def _(pool):
            pool.memset(ones[:, :], 1.0).then_inc(const_set, 1)
            pool.memset(neg_half[:, :], -0.5).then_inc(const_set, 1)
            for u in range(2):
                for h in range(2):
                    pool.memset(T2m[u][h][0:64, :].bitcast(f32), 0.0).then_inc(const_set, 1)
                    pool.memset(T2s[u][h][0:64, :].bitcast(f32), 0.0).then_inc(const_set, 1)
            pool.wait_ge(const_set, 10)
            for u in range(2):
                for h in range(2):
                    pool.memset(T2s[u][h][0:NT, :].bitcast(f32), 1.0).then_inc(const_set, 1)

            def inverse_root(n):
                pool.wait_ge(var_done, n + 1)
                pool.tensor_tensor(rstd[:, :], ve[:, :], neg_half[:, :], ALU.pow).then_inc(rstd_done, 1)

            inverse_root(0)
            inverse_root(1)
            with pool.Fori(0, B) as b:
                def step(g, p, u, prep, fin):
                    tb = t_at(b, p * T_PAIR)
                    for i in range(2 * NT):
                        half, k = i // NT, i % NT
                        if not prep and i in (9, 14):
                            inverse_root(3 * b + 2 + i // 14)
                        for h in range(2):
                            if k == 0:
                                continue
                            n = 2 * (NT - 1) * half + 2 * (k - 1) + h
                            j = 2 * i + h
                            pool.wait_ge(t_used, tb + j + 1)
                            if k > 1:
                                pool.wait_ge(add_done, ADDS * g + n - 1)
                            sl = acc[:, u, h, half * HALF:(half + 1) * HALF]
                            pool.tensor_tensor(sl, Pt[:, (j - 2) % P_RING, :] if k == 1 else sl,
                                               Pt[:, j % P_RING, :], ALU.add).then_inc(add_done, 1)

                steps(pool, b, step)
                inverse_root(3 * b + 4)

        @block.vector
        def _(dve):
            dve.wait_ge(const_in, 16 * LOADS)
            dve.wait_ge(exp_c, 1)
            dve.tensor_scalar(e_c[:, :], e_c[:, :], 1.0, None, ALU.add).then_inc(setup, 1)
            dve.wait_ge(setup, 1)
            dve.reciprocal(silu_c[:, :], e_c[:, :]).then_inc(setup, 1)
            dve.wait_ge(setup, 2)
            dve.tensor_tensor(silu_c[:, :], silu_c[:, :], c_sb[:, :], ALU.mult).then_inc(silu_done, 1)
            dve.wait_ge(mod_mm, 1)
            for n in range(3):
                dve.tensor_copy(modr[:, n * HALF:(n + 1) * HALF], MB[n][0:B, :]).then_inc(setup, 1)
            dve.tensor_copy(mod_t[:, 0:KD, :],
                            TB[0][:, 0:KD * B].rearrange("p (k b) -> p k b", b=B)).then_inc(setup, 1)
            dve.tensor_scalar(mod_t[:, KD:2 * KD, :],
                              TB[0][:, KD * B:2 * KD * B].rearrange("p (k b) -> p k b", b=B),
                              1.0, None, ALU.add).then_inc(setup, 1)
            dve.wait_ge(setup, 7)
            ca = modr[:, D:2 * D]
            dve.tensor_scalar(ca, ca, 1.0, None, ALU.add).then_inc(rows_done, 1)
            for n, m in enumerate((2, 5)):
                row, sign, size = modr[:, m * D:(m + 1) * D], guard[:, 2 * n, :], guard[:, 2 * n + 1, :]
                dve.tensor_scalar(size, row, -1.0, None, ALU.mult).then_inc(setup, 1)
                dve.tensor_scalar(sign, row, 0.0, 2.0, ALU.is_ge, ALU.mult).then_inc(setup, 1)
                dve.wait_ge(setup, 9 + 4 * n)
                dve.tensor_tensor(size, size, row, ALU.max).then_inc(setup, 1)
                dve.tensor_scalar(sign, sign, -1.0, None, ALU.add).then_inc(setup, 1)
                dve.wait_ge(setup, 11 + 4 * n)
                dve.scalar_tensor_tensor(out=row, in0=size, scalar=0.25, in1=sign, op0=ALU.max,
                                         op1=ALU.mult).then_inc(rows_done, 1)

            def layer_norm(ln, src, dst):
                for t in range(NT):
                    dve.bn_stats(stats[:, t, :], src[:, t, :]).then_inc(stats_done, 1)
                dve.wait_ge(stats_done, NT * ln + NT)
                me, qe, mo, qo = (stats[:, :, i] for i in (1, 2, 4, 5))
                dve.tensor_tensor(mv[:, :, 0], me, mo, ALU.add).then_inc(merged, 1)
                dve.tensor_tensor(mv[:, :, 1], me, mo, ALU.subtract).then_inc(merged, 1)
                dve.tensor_tensor(ve[:, :], qe, qo, ALU.add).then_inc(merged, 1)
                dve.wait_ge(merged, 6 * ln + 3)
                dve.tensor_scalar(mv[:, :, 0], mv[:, :, 0], 0.5, None, ALU.mult).then_inc(merged, 1)
                dve.scalar_tensor_tensor(out=mv[:, :, 1], in0=mv[:, :, 1], scalar=0.25, in1=mv[:, :, 1],
                                         op0=ALU.mult, op1=ALU.mult).then_inc(merged, 1)
                dve.tensor_scalar(ve[:, :], ve[:, :], 1.0 / D, EPS, ALU.mult, ALU.add).then_inc(merged, 1)
                dve.wait_ge(merged, 6 * ln + 6)
                dve.tensor_tensor(ve[:, :], ve[:, :], mv[:, :, 1], ALU.add).then_inc(var_done, 1)
                dve.wait_ge(rstd_done, ln + 1)
                for t in range(NT):
                    dve.tensor_scalar(dst[:, t, :], src[:, t, :], mv[:, t, 0:1], rstd[:, t:t + 1],
                                      ALU.subtract, ALU.mult).then_inc(normed, 1)

            def row(rows, j, n=NT):
                return rows[:, j:j + 1, :].broadcast_to([P, n, D])

            def first_norm(n):
                dve.wait_ge(x_in, 64 * n + 64)
                layer_norm(3 * n - 1 if b_given(n) else 0, xt, hbuf)
                dve.wait_ge(normed, 24 * n if b_given(n) else 8)
                dve.tensor_tensor(hbuf[:, :, :], hbuf[:, :, :], row(mod_a, 1), ALU.mult).then_inc(modulated, 1)
                dve.wait_ge(modulated, 4 * n + 1)
                dve.tensor_tensor(hbuf[:, :, :], hbuf[:, :, :], row(mod_a, 0), ALU.add).then_inc(modulated, 1)
                dve.wait_ge(modulated, 4 * n + 2)

            def second_norm(n):
                layer_norm(3 * n if b_given(n) else 1, hbuf, nbuf)
                dve.wait_ge(normed, 24 * n + 8 if b_given(n) else 16)
                dve.tensor_tensor(hbuf[:, :, :], hbuf[:, :, :], row(mod_a, 2), ALU.mult).then_inc(modulated, 1)
                dve.wait_ge(modulated, 4 * n + 3)
                dve.tensor_tensor(xt[:, :, :], xt[:, :, :], hbuf[:, :, :], ALU.add).then_inc(modulated, 1)

            def filled(base, j):
                dve.wait_ge(m_ready, base + j + 1)
                return MB[j % M_RING]

            def rotate(base, j, n):
                kind, half, swap = n // 4, n // 2 % 2, n % 2
                sl = slice(half * HALF, (half + 1) * HALF)
                dst = tmp[:, half, :] if swap else rot[:, kind, sl]
                dve.tensor_tensor(dst, filled(base, j)[:, :], cos_sin[:, swap, sl], ALU.mult)\
                    .then_inc(m_used, 1)
                if swap:
                    dve.wait_ge(m_used, base + j + 1)
                    dve.tensor_tensor(rot[:, kind, sl], rot[:, kind, sl], tmp[:, half, :], ALU.add)\
                        .then_inc(rope_done, 1)

            def low(n, g, u):
                h, kind = n % 2, n // 2
                dve.wait_ge(hi_done, 8 * g + (1, 4, 5, 8)[n])
                rows = slice(64 * h, 64 * h + 64)
                high = (T1m[u][0], T2m[u][1], T1s[u][0], T1s[u][1])[n][rows, :]
                dst = (T1m if kind == 0 else T2s)[u][h][64:128, :]
                dve.tensor_tensor(dst, rot[rows, kind, :], high.bitcast(f32), ALU.subtract)\
                    .then_inc(lo_done, 1)

            def maxima(base, j, n):
                part, m = n // (2 * NT), n % (2 * NT)
                dve.tensor_reduce(mxp[:, part, m // 2, m % 2:m % 2 + 1], filled(base, j)[:, :], AX.X, ALU.max)\
                    .then_inc(m_used, 1)

            def rows_of_maxima(base, j, part, u):
                dve.wait_ge(m_used, base + j)
                dve.tensor_reduce(mx[:, part, :], mxp[:, part, :, :], AX.X, ALU.max).then_inc(max_done, 1)
                bank = filled(base, j)
                for h in range(2):
                    wrote = dve.tensor_tensor(T2m[u][h][0:NT, part * HALF:(part + 1) * HALF]
                                              .rearrange("t (a n) -> t a n", n=P),
                                              bank[0:NT, 0:P].rearrange("t (a n) -> t a n", a=1)
                                              .broadcast_to([NT, TPH, P]),
                                              diag[:, TPH * h:TPH * (h + 1)].rearrange("t (a n) -> t a n", n=1)
                                              .broadcast_to([NT, TPH, P]), ALU.mult)
                wrote.then_inc(m_used, 1)

            def take_sums(base, j):
                for half in range(NHALF):
                    dve.tensor_copy(sums[:, half * HALF:(half + 1) * HALF], filled(base, j + half)[:, :])\
                        .then_inc(m_used, 1)

            def invert(g):
                dve.wait_ge(cs_in, 32 * g)
                dve.reciprocal(rc[:, :, :], cs[:, :, :]).then_inc(inv_done, 1)

            def normalise(g, p):
                dve.wait_ge(rb_in, 32 * g)
                dve.wait_ge(o_used, 2 * g)
                sl = VS[:, bass.ds(p, 1), :]
                dve.tensor_tensor(sl, sl, rb[:, :].rearrange("p (a n) -> p a n", a=1), ALU.mult)\
                    .then_inc(norm_done, 1)

            first_norm(0)
            second_norm(0)
            for n in range(M_PROJ):
                rotate(0, n, n)
            for n in range(4):
                low(n, 0, 0)
            for n in range(M_MAX):
                maxima(0, M_PROJ + n, n)
            for part in range(2):
                rows_of_maxima(0, M_PROJ + M_MAX + part, part, 0)

            with dve.Fori(0, B) as b:
                def step(g, p, u, prep, fin):
                    mb = m_base(b, p)
                    if not fin:
                        for i in range(2):
                            dve.wait_ge(stored[i], 32 * b + 16)
                    for j, (_, what, n) in enumerate(step_units(prep, fin)):
                        if what == "proj":
                            rotate(mb, j, n)
                        elif what == "sum":
                            dve.tensor_copy(sums[:, n * HALF:(n + 1) * HALF], filled(mb, j)[:, :])\
                                .then_inc(m_used, 1)
                        elif what == "max2":
                            maxima(mb, j, M_MAX // 2 + n)
                            if prep and n == LOWS_AT:
                                low(0, g + 1, 1 - u)
                                low(1, g + 1, 1 - u)
                        elif what == "rows2":
                            rows_of_maxima(mb, j, 1, u)
                        elif what == "max1":
                            if n == 0 and not fin:
                                low(0, g + 1, 1 - u)
                                low(1, g + 1, 1 - u)
                            maxima(mb, j, n)
                            if n in (3, 7):
                                low(2 + n // 7, g + 1, 1 - u)
                            if fin and n == 5:
                                invert(g)
                            if fin and n == 12:
                                normalise(g, p - 1)
                        else:
                            rows_of_maxima(mb, j, 0, 1 - u)
                    if not prep:
                        first_norm(b + 1)
                        invert(g)
                        second_norm(b + 1)
                        normalise(g, p - 1)

                steps(dve, b, step)
                take_sums(m_at(b, M_FIN), 0)
                invert(8 * b + NP)
                normalise(8 * b + NP, NP - 1)

                dve.tensor_copy(mod_c[:, :, :], mod_t[:, :, bass.ds(b, 1)]).then_inc(cols_done, 1)
                dve.wait_ge(base_in, 48 * b + 48)
                mo = m_at(b, M_OUT)
                for w in range(NT // 2):
                    if w >= 2:
                        dve.wait_ge(x1_done, 4 * b + w - 1)
                    bank = filled(mo, w)
                    dve.tensor_tensor(obuf[:, w % 2, :, :], bank[:, :].rearrange("p (t d) -> p t d", d=D),
                                      row(mod_b, 0, 2), ALU.mult).then_inc(m_used, 1)
                    dve.wait_ge(m_used, mo + w + 1)
                    sl = xres[:, 2 * w:2 * w + 2, :]
                    dve.tensor_tensor(sl, sl, obuf[:, w % 2, :, :], ALU.add).then_inc(x1_done, 1)
                dve.wait_ge(x1_done, 4 * b + 4)
                layer_norm(3 * b + 4, xres, n2buf)

                for n in range(M_PROJ):
                    rotate(m_at(b, M_PROJ0), n, n)

                dve.wait_ge(t_used, t_at(b, T_TR2 + T_TR))
                dve.tensor_scalar(sodd[:, :, :], h3T[:, :, 2:2 + 4 * LORA:2], ls_bc[:, 0:1], None, ALU.mult)\
                    .then_inc(odd_done, 1)
                for k in range(KD):
                    dve.tensor_tensor(D_sb[:, k, :, :],
                                      ident[:, :].rearrange("p (a n) -> p a n", a=1)
                                      .broadcast_to([P, 2 * LORA, P]),
                                      h3T[:, k, 1:1 + 4 * LORA:2].rearrange("p (a n) -> p a n", n=1)
                                      .broadcast_to([P, 2 * LORA, P]), ALU.mult).then_inc(spread_done, 1)
                dve.wait_ge(odd_done, b + 1)
                dve.wait_ge(wc_in, 32 * b + 32)
                for j in range(4):
                    second, k = j // 2, j % 2
                    bank = filled(m_at(b, M_LORA), j)
                    for i in range(LORA):
                        even = bank[:, i * P:(i + 1) * P]
                        for s in range(KD):
                            if second:
                                dst = w2_sb[:, s:NH:KD, 64 * i + 32 * k:64 * i + 32 * k + 32]
                                src = even.rearrange("p (a c) -> p c a", c=4)
                            else:
                                dst = w1_sb[:, s, D * i + P * k:D * i + P * (k + 1)]
                                src = even
                            last = dve.scalar_tensor_tensor(
                                out=dst, in0=src, scalar=sodd[:, s, LORA * second + i:LORA * second + i + 1],
                                in1=dst, op0=ALU.mult, op1=ALU.add)
                    last.then_inc(m_used, 1)

                for n in range(4):
                    low(n, 8 * b + 8, 0)
                mt, j = m_at(b, M_TAIL), 0
                for what, *n in TAIL:
                    if what == "ffn2":
                        w, = n
                        o = obuf[:, w % 2, :, :]
                        if w >= 2:
                            dve.wait_ge(stored[w % 2], 16 + 32 * b + 16 * (w // 2))
                        bank = filled(mt, j)
                        j += 1
                        dve.tensor_tensor(o, bank[:, :].rearrange("p (t d) -> p t d", d=D),
                                          b2_bc[:, :].rearrange("p (a d) -> p a d", a=1).broadcast_to([P, 2, D]),
                                          ALU.add).then_inc(m_used, 1)
                        dve.wait_ge(m_used, mt + j)
                        dve.tensor_tensor(o, o, row(mod_b, 1, 2), ALU.mult).then_inc(gated, 1)
                        dve.wait_ge(gated, 4 * b + w + 1)
                        dve.tensor_tensor(o, o, xres[:, 2 * w:2 * w + 2, :], ALU.add).then_inc(out_ready, 1)
                    elif what == "max":
                        for m in range(*n):
                            maxima(mt, j, m)
                            j += 1
                    elif what == "rows":
                        for part in range(2):
                            rows_of_maxima(mt, j, part, 0)
                            j += 1


def kernel(**inputs):
    import numpy as np
    import concourse.bacc as bacc
    from concourse.bass_utils import run_bass_kernel_spmd

    a = {n.removeprefix("L0_"): np.asarray(v) for n, v in inputs.items()}

    inv_freq = 1.0 / 10000.0 ** (np.arange(0, DH, 2, dtype=np.float32) / DH)
    freqs = np.outer(np.arange(S, dtype=np.float32), inv_freq)
    cos = np.concatenate([np.cos(freqs), np.cos(freqs)], -1)[:, ::2].T
    sin = np.concatenate([np.sin(freqs), np.sin(freqs)], -1)[:, ::2].T
    signed = np.stack([-sin, sin], 1)
    rope = np.stack([np.tile(np.repeat(cos, 2, 0), (2, 1)),
                     np.tile(signed.reshape(DH, S), (2, 1))], 1).astype(np.float32)

    def pairs(w):
        return w.reshape(NP, P, R).transpose(0, 2, 1)

    def swapped(w):
        return w.reshape(-1, 2, R)[:, ::-1, :].reshape(w.shape)

    def tiles(w):
        return w.reshape(-1, P, w.shape[1]).transpose(1, 0, 2)

    wq, wk = a["attn_w_up_q"], a["attn_w_up_k"]
    arrays = {
        "x": a["attn_x"],
        "w_pair": np.stack([pairs(wq), pairs(swapped(wq)), pairs(wk), pairs(swapped(wk))], 2),
        "w_v": a["attn_w_up_v"].T,
        "w_down": np.stack([tiles(a["attn_w_down_q"].T), tiles(a["attn_w_down_kv"].T)], 2),
        "w_out": tiles(a["attn_w_out"].T),
        "w1": tiles(a["ffn_W1"].T),
        "w2": tiles(a["ffn_W2"].T),
        "ln_cols": np.concatenate([a["attn_ln_scale"].reshape(KD, P), a["attn_ln_bias"].reshape(KD, P)]).T,
        "b1_cols": a["ffn_b1"].reshape(NH, P).T,
        "b2": a["ffn_b2"].reshape(1, D),
        "lora_scale": a["ffn_scale"].reshape(1, 1),
        "c_cols": tiles(a["c"].T).reshape(P, KD * B),
        "w_mod": tiles(a["wmod"]),
        "rope": rope,
        "ident_in": np.eye(P, dtype=np.float32),
        "diag_in": -np.eye(NT, dtype=np.float32),
    }
    nc = bacc.Bacc("TRN2", target_bir_lowering=False, num_devices=1)
    args, sent = {}, {}
    for name, v in arrays.items():
        v = np.ascontiguousarray(v)
        sent[f"in_{name}"] = v
        args[name] = nc.dram_tensor(f"in_{name}", v.shape, mybir.dt.from_np(v.dtype), kind="ExternalInput").ap()
    args["out"] = nc.dram_tensor("out_0", (B, S, D), mybir.dt.float32, kind="ExternalOutput").ap()
    build(nc, **args)
    return run_bass_kernel_spmd(nc, [sent], core_ids=[0]).results[0]["out_0"]
```

```python
from contextlib import ExitStack

import concourse.bass as bass
from concourse import mybir

B, S, D = 8, 1024, 256
H, DH = 16, 64
R = 128
HID = 1024
P = 128
NP = H // 2
NT = S // P
KD = D // P
NH = HID // P
HALF = 512
NHALF = S // HALF
TPH = HALF // P
LORA = 4
EPS = 1e-5
SCALE = DH ** -0.5

M_RING = 3
M_SUM, M_MAX, M_ROW = 2, 4 * NT, 2


M_MAX1 = M_MAX // 2 + 4
M_MAX2 = M_MAX - M_MAX1
STEP = [(slot, "max2", n) for n, slot in enumerate((0, 0, 1, 1, 2, 2, 3, 3, 4))] + \
       [(None, "rope", 0), (None, "rope", 1), (6, "max2", 9), (None, "rope", 2),
        (7, "sum", 0), (None, "rope", 3), (8, "sum", 1), (None, "rope", 4), (10, "max2", 10),
        (None, "rope", 5), (11, "max2", 11), (13, "rows2", 1), (None, "low", 0), (None, "low", 1)] + \
       [(17 + n * 11 // 15, "max1", n) for n in range(3)] + [(None, "low", 2)] + \
       [(17 + n * 11 // 15, "max1", n) for n in range(3, 6)] + [(None, "invert", 0), (None, "low", 3)] + \
       [(17 + n * 11 // 15, "max1", n) for n in range(6, 12)] + [(None, "normalise", 0)] + \
       [(17 + n * 11 // 15, "max1", n) for n in range(12, 16)] + \
       [(28, "max1", 16), (29, "rows1", 0), (29, "max1", 17), (30, "max1", 18), (31, "max1", 19)]
AFTER_ROWS1 = len(STEP) - 1 - STEP.index((29, "rows1", 0))


def step_order(prep, fin):
    def there(what):
        return fin if what in ("max2", "rows2", "sum") else fin and prep if what in ("invert", "normalise") else prep
    return [item for item in STEP if there(item[1])]


def step_units(prep, fin):
    return [item for item in step_order(prep, fin) if item[0] is not None]


M_FIRST, M_STEP = len(step_units(True, False)), len(step_units(True, True))
M_BEFORE = M_MAX + M_ROW
assert M_FIRST % M_RING == M_STEP % M_RING == 0
M_LAST = M_FIRST + (NP - 2) * M_STEP
M_FIN = M_LAST + len(step_units(False, True))
M_OUT = M_FIN + M_SUM
M_LORA = M_OUT + NT // 2
M_TAIL = M_LORA + 4
QUARTERS = NT // 2
M_ALL = M_TAIL + M_MAX + M_ROW + QUARTERS
T_RING = 3
T_TR, T_C, T_V = 4, 4, 2 * NT
T_A = T_TR + T_C + T_V
T_PROJ = 4
T_BEFORE = T_A + T_PROJ
T_PAIR = 4 * NT
T_STEP = T_PAIR + T_PROJ
assert T_STEP % T_RING == 0
T_NEXT = (NP - 1) * T_STEP + T_PAIR
T_TR2 = T_NEXT + T_A
T_FFN = T_TR2 + T_TR + T_PROJ
T_ALL = T_FFN + QUARTERS * NH // 2


def t_score(i, h, prep):
    return 2 * i + h + (min(2 * i, T_PROJ) if prep else 0)


def t_proj(n):
    return t_score(n // 2, 1, True) + 1 + n % 2


BANKS = NH // 2


def tail():
    parts, n = [], 0
    for q in range(QUARTERS):
        for bank in range(BANKS):
            parts.append(("ffn1", q, bank))
            if q:
                upto = ((q - 1) * BANKS + bank) * M_MAX // ((QUARTERS - 1) * BANKS - 1)
                parts += [("max", m) for m in range(n, upto)]
                n = upto
        if q:
            parts.append(("ffn2", q - 1))
    return parts + [("rows", 0), ("rows", 1), ("ffn2", QUARTERS - 1)]


TAIL = tail()
TAIL_UNITS = [part for part in TAIL if part[0] != "ffn1"]
P_RING = 8
ADDS = 2 * (NT - 1)
PV = 2 * NT


HIGH_AT = (8, 9, 10, 12, 13, 14, 15, 16)
HIGHS = (0, 1, 3, 4, 5, 6, 7, 2)
ROOT_AT = (6, 12)


def b_given(n):
    return not (isinstance(n, int) and n == 0)


def build(nc, x, w_pair, w_v, w_down, w_out, w1, w2, ln_cols, b1_cols, b2, lora_scale,
          c_cols, w_mod, rope, ident_in, diag_in, out):
    f32, f32r = mybir.dt.float32, mybir.dt.float32r
    ALU, ACT, AX = mybir.AluOpType, mybir.ActivationFunctionType, mybir.AxisListType

    mod_d = nc.dram_tensor("mod_rows", [B, 6 * D], f32, kind="Internal").ap()
    base_d = nc.dram_tensor("first_base", [P, NT, D], f32, kind="Internal").ap()
    inv_d = nc.dram_tensor("inverse_sums", [2, S], f32, kind="Internal").ap()

    ctx = ExitStack()
    with ctx:
        def sb(name, shape, dt=f32, stack=ctx):
            return stack.enter_context(nc.sbuf_tensor(name, shape, dt))

        def sem(name):
            return ctx.enter_context(nc.semaphore(name))

        ident = sb("ident", [P, P])
        ones = sb("ones", [P, P])
        diag = sb("diag", [NT, NT])
        neg_half = sb("neg_half", [P, NT])
        ln_t = sb("ln_t", [P, 2 * KD])
        b1_t = sb("b1_t", [P, NH])
        b2_bc = sb("b2_bc", [P, D])
        ls_bc = sb("ls_bc", [P, 1])
        mod_t = sb("mod_t", [P, 2 * KD, B])
        mod_c = sb("mod_c", [P, 2 * KD, 1])
        cos_sin = sb("cos_sin", [P, 2, S])
        wo = sb("wo", [P, NP, D])
        mod_a = sb("mod_a", [P, 3, D])
        mod_b = sb("mod_b", [P, 2, D])
        wd = sb("wd", [P, KD, 2, R])
        xres = sb("xres", [P, NT, D])
        cT = sb("cT", [P, 2, S])
        VS = sb("VS", [P, NP, S])
        wp = [sb(f"wp{u}", [P, 2, P]) for u in range(2)]
        sums = sb("sums", [P, S])
        rb = sb("rb", [P, S])
        cs = sb("cs", [P, 2, NT])
        rc = sb("rc", [P, 2, NT])
        stats = sb("stats", [P, NT, 6])
        mv = sb("mv", [P, NT, 2])
        ve = sb("ve", [P, NT])
        rstd = sb("rstd", [P, NT])
        mxp = sb("mxp", [P, NHALF, NT, 2])
        mx = sb("mx", [P, NHALF, NT])
        sodd = sb("sodd", [P, KD, 2 * LORA])
        T2m = [[sb(f"T2m{u}{h}", [P, S], f32r) for h in range(2)] for u in range(2)]
        T2s = [[sb(f"T2s{u}{h}", [P, S], f32r) for h in range(2)] for u in range(2)]

        def shared(*layouts):
            made = []
            for n, layout in enumerate(layouts):
                stack = ctx if n == len(layouts) - 1 else ExitStack()
                made += [sb(name, shape, dt, stack) for name, shape, dt in layout]
                if n < len(layouts) - 1:
                    stack.close()
            return made

        xt, hbuf, *t1 = shared(
            [("xt", [P, NT, D], f32), ("hbuf", [P, NT, D], f32)],
            [(f"T1{k}0{h}", [P, S], f32r) for k in "ms" for h in range(2)])
        hT, hid, *t2 = shared([("hT", [P, KD, S], f32)], [("hid", [P, 2, NH, 2 * P], f32)],
                          [(f"T1{k}1{h}", [P, S], f32r) for k in "ms" for h in range(2)])
        T1m, T1s = [t1[0:2], t2[0:2]], [t1[2:4], t2[2:4]]
        w1_sb, w2_sb, Pt = shared(
            [("w1_sb", [P, KD, HID], f32), ("w2_sb", [P, NH, D], f32)],
            [("Pt", [P, P_RING, HALF], f32)])
        n2buf, D_sb, acc = shared(
            [("n2buf", [P, NT, D], f32), ("D_sb", [P, KD, 2 * LORA, P], f32)],
            [("acc", [P, 2, 2, S], f32)])
        wv, h3T, Vp0, Vp1 = shared([("wv", [P, H * DH], f32)], [("h3T", [P, KD, S], f32)],
                                   [("Vp0", [P, NT, P], f32), ("Vp1", [P, NT, P], f32)])
        Vp = [Vp0, Vp1]
        nbuf, rot = shared([("nbuf", [P, NT, D], f32)], [("rot", [P, 2, S], f32)])
        obuf, swapped = shared([("obuf", [P, 2, 2, D], f32)], [("swapped", [P, 2, S], f32)])
        c_sb, e_c, silu_c = (sb(n, [P, KD * B]) for n in ("c_sb", "e_c", "silu_c"))
        wm = VS[:, 0:3, :].rearrange("p a s -> p (a s)").rearrange("p (k n) -> p k n", k=KD)
        modr = VS[0:B, 3:5, :].rearrange("p a s -> p (a s)")[:, 0:6 * D]
        guard = VS[0:B, 5, :].rearrange("p (k d) -> p k d", d=D)

        MB = [ctx.enter_context(nc.psum_tensor(f"M{i}", [P, HALF], f32)) for i in range(M_RING)]
        TB = [ctx.enter_context(nc.psum_tensor(f"T{i}", [P, HALF], f32)) for i in range(T_RING)]
        OB = [ctx.enter_context(nc.psum_tensor(f"O{i}", [P, HALF], f32)) for i in range(2)]

        mod_in = sem("mod_in")
        const_in = sem("const_in")
        const_set = sem("const_set")
        setup = sem("setup")
        exp_c, silu_done = sem("exp_c"), sem("silu_done")
        mod_mm = sem("mod_mm")
        rows_done = sem("rows_done")
        m_ready = sem("m_ready")
        m_used = sem("m_used")
        t_ready = sem("t_ready")
        t_used = sem("t_used")
        swap_in = [sem("swap_in_q"), sem("swap_in_k")]
        turned = sem("turned")
        rope_done = sem("rope_done")
        hi_done = sem("hi_done")
        lo_done = sem("lo_done")
        max_done = sem("max_done")
        pv_done = sem("pv_done")
        add_done = sem("add_done")
        o_used = sem("o_used")
        inv_done = sem("inv_done")
        quarter_inv = sem("quarter_inv")
        norm_done = sem("norm_done")
        x_in = sem("x_in")
        wv_in = sem("wv_in")
        base_out, base_in = sem("base_out"), sem("base_in")
        wc_in = sem("wc_in")
        wp_in = [sem(f"wp_in{u}") for u in range(2)]
        v_in = [sem(f"v_in{u}") for u in range(2)]
        cs_in, inv_out, rb_in = sem("cs_in"), sem("inv_out"), sem("rb_in")
        stats_done, merged, var_done = sem("stats_done"), sem("merged"), sem("var_done")
        rstd_done = sem("rstd_done")
        normed = sem("normed")
        modulated = sem("modulated")
        cols_done = sem("cols_done")
        x1_done = sem("x1_done")
        odd_done, spread_done = sem("odd_done"), sem("spread_done")
        gated = sem("gated")
        out_ready = sem("out_ready")
        stored = [sem(f"stored{i}") for i in range(2)]

        LOADS = 9

        block = ctx.enter_context(nc.Block())

        def steps(eng, b, step):
            step(8 * b, 0, 0, True, False)
            with eng.Fori(0, (NP - 2) // 2) as i:
                for r in (1, 2):
                    step(8 * b + (2 * i + r), 2 * i + r, r % 2, True, True)
            step(8 * b + NP - 1, NP - 1, (NP - 1) % 2, False, True)

        def m_at(b, offset):
            return M_BEFORE + b * M_ALL + offset

        def m_base(b, p):
            if isinstance(p, int) and p == 0:
                return m_at(b, 0)
            return m_at(b, M_FIRST + (p - 1) * M_STEP)

        def last_sum(prep):
            return 1 + max(n for n, (_, what, _) in enumerate(step_units(prep, True)) if what == "sum")

        def t_at(b, offset):
            return T_BEFORE + b * T_ALL + offset

        @block.sync
        def _(sp):
            def load_x(b):
                sp.dma_start(xt[:, :, :], x[bass.ds(b, 1), :, :].rearrange("a (t p) d -> p (a t) d", p=P))\
                    .then_inc(x_in, 16)

            sp.dma_start(c_sb[:, :], c_cols).then_inc(mod_in, 16)
            sp.dma_start(wm, w_mod).then_inc(mod_in, 16)
            load_x(0)
            for dst, src in ((ident[:, :], ident_in), (diag[:, :], diag_in), (ln_t[:, :], ln_cols),
                             (b1_t[:, :], b1_cols), (b2_bc[:, :], b2.partition_broadcast(P)),
                             (ls_bc[:, :], lora_scale.partition_broadcast(P)),
                             (cos_sin[:, :, :], rope), (wo[:, :, :], w_out), (wd[:, :, :, :], w_down)):
                sp.dma_start(dst, src).then_inc(const_in, 16)
            sp.wait_ge(rows_done, 3)
            for i in range(2):
                half = slice(i * B // 2, (i + 1) * B // 2)
                sp.dma_start(mod_d[half, :], modr[half, :]).then_inc(stored[i], 16)
            for i in range(2):
                sp.wait_ge(stored[i], 16)

            def finish(n, m_sums):
                sp.wait_ge(m_used, m_sums)
                for h in range(2):
                    sp.dma_start(cs[:, h, :], sums[64 * h:64 * h + 1, :]).then_inc(cs_in, 16)
                sp.wait_ge(inv_done, n)
                for h in range(2):
                    sp.dma_start(inv_d[h, :].rearrange("(p j) -> p j", p=P), rc[:, h, :]).then_inc(inv_out, 16)
                sp.wait_ge(inv_out, 32 * n)
                for h in range(2):
                    sp.dma_start(rb[64 * h:64 * h + 64, :], inv_d[h:h + 1, :].partition_broadcast(64))\
                        .then_inc(rb_in, 16)

            def load_a(b):
                for m in range(3):
                    sp.dma_start(mod_a[:, m:m + 1, :],
                                 mod_d[bass.ds(b, 1), m * D:(m + 1) * D].partition_broadcast(P))\
                        .then_inc(x_in, 16)
                sp.dma_start(wv[:, :], w_v).then_inc(wv_in, 16)
                for u in range(2):
                    sp.dma_start(wp[u][:, :, :], w_pair[u]).then_inc(wp_in[u], 16)

            def load_b(b, done=None):
                sp.dma_start(xres[:, :, :], base_d).then_inc(base_in, 16)
                for j, m in enumerate((2, 5)):
                    if done is not None:
                        sp.wait_ge(stored[j], done)
                    sp.dma_start(mod_b[:, j:j + 1, :],
                                 mod_d[bass.ds(b, 1), m * D:(m + 1) * D].partition_broadcast(P))\
                        .then_inc(base_in, 16)

            def exchange(kind, projected):
                sp.wait_ge(t_used, projected)
                for a in range(2):
                    sp.dma_start(swapped[a:P:2, kind, :], rot[1 - a:P:2, kind, :]).then_inc(swap_in[kind], 16)

            load_a(0)
            sp.wait_ge(modulated, 4)
            sp.dma_start(base_d, xt[:, :, :]).then_inc(base_out, 16)
            sp.wait_ge(base_out, 16)
            load_b(0)
            for kind in range(2):
                exchange(kind, T_TR + T_C + 2 * kind + 2)
            sp.wait_ge(t_used, T_BEFORE)
            for u in range(2):
                sp.dma_start(Vp[u][:, :, :], VS[:, u, :]).then_inc(v_in[u], 16)

            with sp.Fori(0, B) as b:
                after = (b + 1) % B

                def step(g, p, u, prep, fin):
                    if prep and fin:
                        sp.wait_ge(pv_done, PV * g - PV + 1)
                        sp.dma_start(wp[1 - u][:, :, :], w_pair[bass.ds(p + 1, 1), :, :, :]
                                     .rearrange("a p k n -> p (a k) n")).then_inc(wp_in[1 - u], 16)
                    if prep:
                        for kind in range(2):
                            exchange(kind, t_at(b, p * T_STEP) + t_proj(2 * kind + 1) + 1)
                    if prep and fin:
                        sp.wait_ge(pv_done, PV * g)
                        sp.dma_start(Vp[1 - u][:, :, :], VS[:, bass.ds(p + 1, 1), :]).then_inc(v_in[1 - u], 16)
                    if not prep:
                        sp.wait_ge(pv_done, PV * g)
                        load_x(after)
                        load_a(after)
                    if fin:
                        finish((NP - 1) * b + p, m_base(b, p) + last_sum(prep))

                steps(sp, b, step)
                sp.wait_ge(pv_done, PV * 8 * b + PV * NP)
                sp.wait_ge(add_done, ADDS * 8 * b + ADDS * NP)
                sp.dma_start(w1_sb[:, :, :], w1).then_inc(wc_in, 16)
                sp.dma_start(w2_sb[:, :, :], w2).then_inc(wc_in, 16)
                sp.wait_ge(modulated, 4 * b + 8)
                sp.dma_start(base_d, xt[:, :, :]).then_inc(base_out, 16)
                for kind in range(2):
                    exchange(kind, t_at(b, T_TR2 + T_TR + 2 * kind + 2))
                for w in range(QUARTERS):
                    if w == 2:
                        sp.wait_ge(t_used, t_at(b, T_ALL))
                        for u in range(2):
                            sp.dma_start(Vp[u][:, :, :], VS[:, u, :]).then_inc(v_in[u], 16)
                    sp.wait_ge(out_ready, 4 * b + w + 1)
                    sp.dma_start(out[bass.ds(b, 1), 2 * w * P:2 * (w + 1) * P, :]
                                 .rearrange("a (t p) d -> p (a t) d", p=P), obuf[:, w % 2, :, :])\
                        .then_inc(stored[w % 2], 16)
                sp.wait_ge(base_out, 16 * b + 32)
                load_b(after, 32 * b + 48)
            for i in range(2):
                sp.wait_ge(stored[i], 16 + 32 * B)
            sp.wait_ge(base_in, 48 * (B + 1))
            for u in range(2):
                sp.wait_ge(v_in[u], 16 * (4 * B + 1))
                sp.wait_ge(wp_in[u], 16 * (4 * B + 1))

        @block.tensor
        def _(pe):
            pe.wait_ge(mod_in, 32)
            pe.wait_ge(silu_done, 1)
            for n in range(3):
                for k in range(KD):
                    mm = pe.matmul(MB[n][0:B, :], silu_c[:, k * B:(k + 1) * B],
                                   wm[:, k, n * HALF:(n + 1) * HALF], start=(k == 0), stop=(k == KD - 1))
            for j in range(2 * KD):
                for k in range(KD):
                    mm = pe.matmul(TB[0][:, j * B:(j + 1) * B], wm[:, k, 3 * D + j * P:3 * D + (j + 1) * P],
                                   silu_c[:, k * B:(k + 1) * B], start=(k == 0), stop=(k == KD - 1))
            mm.then_inc(mod_mm, 1)
            pe.wait_ge(const_set, 14)
            pe.wait_ge(rows_done, 3)

            def m_bank(base, j, goes_on=False):
                pe.wait_ge(m_used, base + (j - M_RING + 1) if j >= M_RING or goes_on else base)
                return MB[j % M_RING]

            def t_bank(base, j, goes_on=False):
                if j >= T_RING or goes_on:
                    pe.wait_ge(t_used, base + (j - T_RING + 1))
                elif not (isinstance(base, int) and base == 0):
                    pe.wait_ge(t_used, base)
                return TB[j % T_RING]

            def transposes(base, j, src):
                k, half = j // NHALF, j % NHALF
                bank = t_bank(base, j)
                for c in range(TPH):
                    mm = pe.transpose(bank[:, c * P:(c + 1) * P],
                                      src[:, TPH * half + c, k * P:(k + 1) * P], ident[:, :])
                mm.then_inc(t_ready, 1)

            def low_rank(base, between=None):
                for j in range(T_TR):
                    transposes(base, j, nbuf)
                pe.wait_ge(t_used, base + T_TR)
                for j in range(T_C):
                    if between and j == 1:
                        between()
                    kind, half = j // 2, j % 2
                    bank = t_bank(base + T_TR, j)
                    for k in range(KD):
                        mm = pe.matmul(bank[:, :], wd[:, k, kind, :], hT[:, k, half * HALF:(half + 1) * HALF],
                                       start=(k == 0), stop=(k == KD - 1))
                    mm.then_inc(t_ready, 1)

            def v_of(base):
                pe.wait_ge(t_used, base)
                for j in range(T_V):
                    t, f = j // 2, j % 2
                    pe.matmul(t_bank(base, j)[:, :], cT[:, 1, t * P:(t + 1) * P], wv[:, f * HALF:(f + 1) * HALF],
                              start=True, stop=True).then_inc(t_ready, 1)

            def proj(bank, n, g, u):
                if n == 0:
                    pe.wait_ge(wp_in[u], 8 * (g - u) + 16)
                kind, half = n // 2, n % 2
                pe.matmul(bank[:, :], wp[u][:, kind, :], cT[:, kind, half * HALF:(half + 1) * HALF],
                          start=True, stop=True).then_inc(t_ready, 1)

            def scores_max(bank, n, g, u):
                if n == 0:
                    pe.wait_ge(hi_done, 8 * g + 7)
                    pe.wait_ge(lo_done, 4 * g + 2)
                part, t, h, half = n // (2 * NT), n // 4 % TPH, n // 2 % 2, n % 2
                t += TPH * part
                pe.matmul(bank[:, :], T1m[u][h][:, t * P:(t + 1) * P],
                          T1s[u][h][:, half * HALF:(half + 1) * HALF],
                          start=True, stop=True).then_inc(m_ready, 1)

            def max_rows(bank, part, g):
                pe.wait_ge(max_done, 2 * g + part + 1)
                pe.transpose(bank[0:NT, 0:P], mx[:, part, :], ident[:, :])\
                    .then_inc(m_ready, 1)

            def sum_rows(bank, half, g, u):
                pe.wait_ge(add_done, ADDS * g + ADDS)
                for h in range(2):
                    mm = pe.matmul(bank[64 * h:64 * h + 64, :], ones[:, 0:64],
                                   acc[:, u, h, half * HALF:(half + 1) * HALF], start=True, stop=True)
                mm.then_inc(m_ready, 1)

            pe.wait_ge(const_in, 16 * LOADS)
            pe.wait_ge(normed, 2 * NT)
            low_rank(0)
            for n in range(T_PROJ):
                proj(t_bank(T_TR + T_C, n), n, 0, 0)
            pe.wait_ge(wv_in, 16)
            v_of(T_TR + T_C + T_PROJ)
            for n in range(M_MAX):
                scores_max(m_bank(0, n), n, 0, 0)
            for h in range(2):
                max_rows(m_bank(0, M_MAX + h), h, 0)

            with pe.Fori(0, B) as b:
                def step(g, p, u, prep, fin):
                    mb, tb = m_base(b, p), t_at(b, p * T_STEP)
                    units = step_units(prep, fin)
                    rows2 = [what for _, what, _ in units].index("rows2") if fin else 0

                    def work(j, what, n):
                        bank = m_bank(mb, j, fin)
                        if what == "sum":
                            sum_rows(bank, n, g - 1, 1 - u)
                        elif what == "max1":
                            scores_max(bank, n, g + 1, 1 - u)
                        elif what == "max2":
                            scores_max(bank, M_MAX1 + n, g, u)
                        elif what == "rows1":
                            max_rows(bank, 0, g + 1)
                        else:
                            max_rows(bank, 1, g)

                    def values(i):
                        half, k = i // NT, i % NT
                        pe.wait_ge(t_used, tb + t_score(i, 1, prep) + 1)
                        if k == 0 and fin:
                            pe.wait_ge(o_used, 2 * g - 1 + half)
                        if i == 0:
                            pe.wait_ge(v_in[u], 8 * (g - u) + 16)
                        for h in range(2):
                            mm = pe.matmul(OB[half][64 * h:64 * h + 64, :], Vp[u][:, k, 64 * h:64 * h + 64],
                                           Pt[:, (2 * i + h) % P_RING, :], start=(k == 0), stop=(k == NT - 1))
                        mm.then_inc(pv_done, 1)

                    pe.wait_ge(hi_done, 8 * g + 8)
                    pe.wait_ge(lo_done, 4 * g + 4)
                    for i in range(2 * NT):
                        half, k = i // NT, i % NT
                        if i == 0:
                            pe.wait_ge(m_used, mb - AFTER_ROWS1 if fin else mb)
                        if i == NT and fin:
                            pe.wait_ge(m_used, mb + rows2 + 1)
                        for h in range(2):
                            bank = t_bank(tb, t_score(i, h, prep), fin)
                            q = slice(half * HALF, (half + 1) * HALF)
                            kk = slice(k * P, (k + 1) * P)
                            pe.matmul(bank[:, :], T1s[u][h][:, kk], T1m[u][h][:, q], start=True, stop=False)
                            pe.matmul(bank[:, :], T2s[u][h][:, kk], T2m[u][h][:, q], start=False, stop=True)\
                                .then_inc(t_ready, 1)
                        for slot in range(2):
                            if slot and i:
                                values(i - 1)
                            for j, (at, what, n) in enumerate(units):
                                if at == 2 * i + slot:
                                    work(j, what, n)
                            for n in range(2 * i, 2 * i + 2):
                                if slot == 0 and prep and n < T_PROJ:
                                    proj(t_bank(tb, t_proj(n), fin), n, g + 1, 1 - u)
                    values(2 * NT - 1)

                steps(pe, b, step)

                pe.wait_ge(normed, 3 * NT * b + 4 * NT)
                def last_sums():
                    for n in range(M_SUM):
                        sum_rows(m_bank(m_at(b, M_FIN), n), n, 8 * b + NP - 1, (NP - 1) % 2)

                low_rank(t_at(b, T_NEXT), last_sums)

                for w in range(NT // 2):
                    pe.wait_ge(norm_done, (NP - 1 + NT // 2) * b + NP + w)
                    bank = m_bank(m_at(b, M_OUT), w)
                    for t in range(2):
                        for f in range(NP):
                            mm = pe.matmul(bank[:, t * D:(t + 1) * D], VS[:, f, (2 * w + t) * P:(2 * w + t + 1) * P],
                                           wo[:, f, :], start=(f == 0), stop=(f == NP - 1))
                    mm.then_inc(m_ready, 1)

                pe.wait_ge(wv_in, 16 * b + 32)
                v_of(t_at(b, T_NEXT + T_TR + T_C))

                pe.wait_ge(normed, 3 * NT * b + 5 * NT)
                for j in range(T_TR):
                    transposes(t_at(b, T_TR2), j, n2buf)
                for n in range(T_PROJ):
                    proj(t_bank(t_at(b, T_TR2), T_TR + n), n, 8 * b + 8, 0)
                for j in range(4):
                    second, k = j // 2, j % 2
                    pe.wait_ge(spread_done, KD * b + k + 1)
                    pe.matmul(m_bank(m_at(b, M_LORA), j)[:, :], ones[:, :],
                              D_sb[:, k, LORA * second:LORA * (second + 1), :], start=True, stop=True)\
                        .then_inc(m_ready, 1)
                pe.wait_ge(m_used, m_at(b, M_LORA + 2))
                mt, j = m_at(b, M_TAIL), 0
                for what, n, *more in TAIL:
                    if what == "ffn1":
                        i, = more
                        bank = t_bank(t_at(b, T_FFN), n * BANKS + i)
                        for s in range(2):
                            for k in range(KD):
                                mm = pe.matmul(bank[:, s * 2 * P:(s + 1) * 2 * P],
                                               w1_sb[:, k, (2 * i + s) * P:(2 * i + s + 1) * P],
                                               h3T[:, k, n * 2 * P:(n + 1) * 2 * P],
                                               start=(k == 0), stop=(k == KD - 1))
                        mm.then_inc(t_ready, 1)
                        continue
                    if what == "ffn2":
                        pe.wait_ge(m_used, mt)
                        pe.wait_ge(t_used, t_at(b, T_FFN + (n + 1) * BANKS))
                        bank = m_bank(mt, j)
                        for t in range(2):
                            for f in range(NH):
                                mm = pe.matmul(bank[:, t * D:(t + 1) * D], hid[:, n % 2, f, t * P:(t + 1) * P],
                                               w2_sb[:, f, :], start=(f == 0), stop=(f == NH - 1))
                        mm.then_inc(m_ready, 1)
                    elif what == "max":
                        scores_max(m_bank(mt, j), n, 8 * b + 8, 0)
                    else:
                        max_rows(m_bank(mt, j), n, 8 * b + 8)
                    j += 1

        @block.scalar
        def _(act):
            act.wait_ge(mod_in, 32)
            act.activation(e_c[:, :], c_sb[:, :], ACT.Exp, scale=-1.0).then_inc(exp_c, 1)

            def empty(base, j):
                act.wait_ge(t_ready, base + j + 1)
                return TB[j % T_RING]

            def take_low_rank(base):
                for j in range(T_TR):
                    k, half = j // NHALF, j % NHALF
                    act.activation(hT[:, k, half * HALF:(half + 1) * HALF], empty(base, j)[:, :], ACT.Identity,
                                   bias=ln_t[:, KD + k:KD + k + 1], scale=ln_t[:, k:k + 1]).then_inc(t_used, 1)
                for j in range(T_C):
                    kind, half = j // 2, j % 2
                    act.activation(cT[:, kind, half * HALF:(half + 1) * HALF], empty(base + T_TR, j)[:, :],
                                   ACT.Copy).then_inc(t_used, 1)

            def take_v(base):
                for j in range(T_V):
                    t, f = j // 2, j % 2
                    act.activation(VS[:, f * NP // 2:(f + 1) * NP // 2, t * P:(t + 1) * P],
                                   empty(base, j)[:, :].rearrange("p (f n) -> p f n", n=P),
                                   ACT.Copy).then_inc(t_used, 1)

            def take_proj(n, base, j, g):
                if n == 0 and g is not None:
                    act.wait_ge(hi_done, 8 * g)
                    act.wait_ge(lo_done, 4 * g)
                kind, half = n // 2, n % 2
                act.activation(rot[:, kind, half * HALF:(half + 1) * HALF], empty(base, j)[:, :], ACT.Copy)\
                    .then_inc(t_used, 1)

            def high(i, g, u):
                n = HIGHS[i]
                if n % 4 == 0:
                    act.wait_ge(rope_done, 2 * g + 1 + n // 4)
                h = n % 2 if n < 4 else n // 2 % 2
                src = rot[64 * h:64 * h + 64, n // 4, :]
                if n < 4:
                    dst = T1m[u][h][0:64, :] if n < 2 else T2m[u][h][64:128, :]
                else:
                    dst = T1s[u][h][0:64, :] if n % 2 == 0 else T1s[u][h][64:128, :]
                act.activation(dst, src, ACT.Copy).then_inc(hi_done, 1)

            act.wait_ge(const_in, 16 * LOADS)
            take_low_rank(0)
            for n in range(T_PROJ):
                take_proj(n, T_TR + T_C, n, None)
            take_v(T_TR + T_C + T_PROJ)
            act.wait_ge(base_out, 16)
            for n in range(8):
                high(n, 0, 0)

            with act.Fori(0, B) as b:
                def output(half, g, p):
                    act.wait_ge(pv_done, PV * g + NT * (half + 1))
                    act.activation(VS[:, bass.ds(p, 1), half * HALF:(half + 1) * HALF],
                                   OB[half][:, :].rearrange("p (a n) -> p a n", a=1), ACT.Copy).then_inc(o_used, 1)

                def step(g, p, u, prep, fin):
                    tb = t_at(b, p * T_STEP)
                    for j in range(T_PAIR):
                        h = j % 2
                        bank = empty(tb, t_score(j // 2, h, prep))
                        if fin or j >= P_RING:
                            act.wait_ge(pv_done, PV * g + (j - P_RING) // 2 + 1)
                            i = (j - P_RING) // 2
                            ih, ik = i // NT, i % NT
                            act.wait_ge(add_done, ADDS * g + (NT - 1) * ih + max(ik, 1))
                        act.activation(Pt[:, j % P_RING, :], bank[:, :], ACT.Exp, scale=SCALE).then_inc(t_used, 1)
                        for n in range(j - 1, j + 1):
                            if prep and h and n < T_PROJ:
                                take_proj(n, tb, t_proj(n), g + 1)
                        if fin and j == 3:
                            output(1, g - 1, p - 1)
                        if j == 19:
                            output(0, g, p)
                        if prep and j in HIGH_AT:
                            high(HIGH_AT.index(j), g + 1, 1 - u)

                steps(act, b, step)
                output(1, 8 * b + NP - 1, NP - 1)
                take_low_rank(t_at(b, T_NEXT))
                take_v(t_at(b, T_NEXT + T_TR + T_C))

                act.wait_ge(cols_done, b + 1)
                for j in range(T_TR):
                    k, half = j // NHALF, j % NHALF
                    act.activation(h3T[:, k, half * HALF:(half + 1) * HALF], empty(t_at(b, T_TR2), j)[:, :],
                                   ACT.Identity, bias=mod_c[:, k, :], scale=mod_c[:, KD + k, :]).then_inc(t_used, 1)
                for n in range(T_PROJ):
                    take_proj(n, t_at(b, T_TR2), T_TR + n, 8 * b + 8)
                act.wait_ge(base_out, 16 * b + 32)
                for q in range(QUARTERS):
                    for f in range(0, NH, 2):
                        j = q * BANKS + f // 2
                        bank = empty(t_at(b, T_FFN), j)
                        if q >= 2:
                            act.wait_ge(m_ready, m_at(b, M_TAIL) + TAIL_UNITS.index(("ffn2", q - 2)) + 1)
                        act.activation(hid[:, q % 2, f, :], bank[:, 0:2 * P], ACT.Gelu, bias=b1_t[:, f:f + 1])
                        act.activation(hid[:, q % 2, f + 1, :], bank[:, 2 * P:4 * P], ACT.Gelu,
                                       bias=b1_t[:, f + 1:f + 2]).then_inc(t_used, 1)
                        if q == 0:
                            high(f, 8 * b + 8, 0)
                            high(f + 1, 8 * b + 8, 0)

        @block.gpsimd
        def _(pool):
            pool.memset(ones[:, :], 1.0).then_inc(const_set, 1)
            pool.memset(neg_half[:, :], -0.5).then_inc(const_set, 1)
            for u in range(2):
                for h in range(2):
                    pool.memset(T2m[u][h][0:64, :].bitcast(f32), 0.0).then_inc(const_set, 1)
                    pool.memset(T2s[u][h][0:64, :].bitcast(f32), 0.0).then_inc(const_set, 1)
            pool.wait_ge(const_set, 10)
            for u in range(2):
                for h in range(2):
                    pool.memset(T2s[u][h][0:NT, :].bitcast(f32), 1.0).then_inc(const_set, 1)

            def inverse_root(n):
                pool.wait_ge(var_done, n + 1)
                pool.tensor_tensor(rstd[:, :], ve[:, :], neg_half[:, :], ALU.pow).then_inc(rstd_done, 1)

            inverse_root(0)
            inverse_root(1)
            with pool.Fori(0, B) as b:
                def step(g, p, u, prep, fin):
                    tb = t_at(b, p * T_STEP)
                    for i in range(2 * NT):
                        half, k = i // NT, i % NT
                        if not prep and i in ROOT_AT:
                            inverse_root(3 * b + 2 + ROOT_AT.index(i))
                        if k == 0:
                            continue
                        n, j = (NT - 1) * half + k - 1, 2 * i
                        pool.wait_ge(t_used, tb + t_score(i, 1, prep) + 1)
                        if k > 1:
                            pool.wait_ge(add_done, ADDS * g + n)
                        sl = acc[:, u, :, half * HALF:(half + 1) * HALF]
                        before = (j - 2) % P_RING
                        pool.tensor_tensor(sl, Pt[:, before:before + 2, :] if k == 1 else sl,
                                           Pt[:, j % P_RING:j % P_RING + 2, :], ALU.add).then_inc(add_done, 1)

                steps(pool, b, step)
                inverse_root(3 * b + 4)

        @block.vector
        def _(dve):
            def statistics(ln, src):
                for t in range(NT):
                    dve.bn_stats(stats[:, t, :], src[:, t, :]).then_inc(stats_done, 1)
                dve.wait_ge(stats_done, NT * ln + NT)
                me, qe, mo, qo = (stats[:, :, i] for i in (1, 2, 4, 5))
                dve.tensor_tensor(mv[:, :, 0], me, mo, ALU.add).then_inc(merged, 1)
                dve.tensor_tensor(mv[:, :, 1], me, mo, ALU.subtract).then_inc(merged, 1)
                dve.tensor_tensor(ve[:, :], qe, qo, ALU.add).then_inc(merged, 1)
                dve.wait_ge(merged, 6 * ln + 3)
                dve.tensor_scalar(mv[:, :, 0], mv[:, :, 0], 0.5, None, ALU.mult).then_inc(merged, 1)
                dve.scalar_tensor_tensor(out=mv[:, :, 1], in0=mv[:, :, 1], scalar=0.25, in1=mv[:, :, 1],
                                         op0=ALU.mult, op1=ALU.mult).then_inc(merged, 1)
                dve.tensor_scalar(ve[:, :], ve[:, :], 1.0 / D, EPS, ALU.mult, ALU.add).then_inc(merged, 1)
                dve.wait_ge(merged, 6 * ln + 6)
                dve.tensor_tensor(ve[:, :], ve[:, :], mv[:, :, 1], ALU.add).then_inc(var_done, 1)

            def normalised(ln, src, dst):
                dve.wait_ge(rstd_done, ln + 1)
                for t in range(NT):
                    dve.tensor_scalar(dst[:, t, :], src[:, t, :], mv[:, t, 0:1], rstd[:, t:t + 1],
                                      ALU.subtract, ALU.mult).then_inc(normed, 1)

            def row(rows, j, n=NT):
                return rows[:, j:j + 1, :].broadcast_to([P, n, D])

            def first_statistics(n):
                dve.wait_ge(x_in, 64 * n + 64 if b_given(n) else 16)
                statistics(3 * n - 1 if b_given(n) else 0, xt)

            def first_norm(n):
                if b_given(n):
                    normalised(3 * n - 1, xt, hbuf)
                dve.wait_ge(normed, 24 * n if b_given(n) else 8)
                dve.tensor_tensor(hbuf[:, :, :], hbuf[:, :, :], row(mod_a, 1), ALU.mult).then_inc(modulated, 1)
                dve.wait_ge(modulated, 4 * n + 1)
                dve.tensor_tensor(hbuf[:, :, :], hbuf[:, :, :], row(mod_a, 0), ALU.add).then_inc(modulated, 1)
                dve.wait_ge(modulated, 4 * n + 2)
                statistics(3 * n if b_given(n) else 1, hbuf)

            def second_norm(n):
                normalised(3 * n if b_given(n) else 1, hbuf, nbuf)

            def first_base(n):
                dve.wait_ge(normed, 24 * n + 8 if b_given(n) else 16)
                dve.tensor_tensor(hbuf[:, :, :], hbuf[:, :, :], row(mod_a, 2), ALU.mult).then_inc(modulated, 1)
                dve.wait_ge(modulated, 4 * n + 3)
                dve.tensor_tensor(xt[:, :, :], xt[:, :, :], hbuf[:, :, :], ALU.add).then_inc(modulated, 1)

            def filled(base, j):
                dve.wait_ge(m_ready, base + j + 1)
                return MB[j % M_RING]

            def rotate(n, g):
                kind, stage = n // 3, n % 3
                if stage == 0:
                    dve.wait_ge(swap_in[kind], 32 * g + 32)
                if stage < 2:
                    part = (rot, swapped)[stage]
                    dve.tensor_tensor(part[:, kind, :], part[:, kind, :], cos_sin[:, stage, :], ALU.mult)\
                        .then_inc(turned, 1)
                else:
                    dve.wait_ge(turned, 4 * g + 2 * kind + 2)
                    dve.tensor_tensor(rot[:, kind, :], rot[:, kind, :], swapped[:, kind, :], ALU.add)\
                        .then_inc(rope_done, 1)

            def low(n, g, u):
                h, kind = n % 2, n // 2
                dve.wait_ge(hi_done, 8 * g + (1, 3, 4, 7)[n])
                rows = slice(64 * h, 64 * h + 64)
                high = (T1m[u][0], T2m[u][1], T1s[u][0], T1s[u][1])[n][rows, :]
                dst = (T1m if kind == 0 else T2s)[u][h][64:128, :]
                dve.tensor_tensor(dst, rot[rows, kind, :], high.bitcast(f32), ALU.subtract)\
                    .then_inc(lo_done, 1)

            def maxima(base, j, n):
                part, m = n // (2 * NT), n % (2 * NT)
                row = m // 2 % 2 * TPH + m // 4
                dve.tensor_reduce(mxp[:, part, row, m % 2:m % 2 + 1], filled(base, j)[:, :], AX.X, ALU.max)\
                    .then_inc(m_used, 1)
                if m == 2 * NT - 1:
                    dve.wait_ge(m_used, base + j + 1)
                    dve.tensor_reduce(mx[:, part, :], mxp[:, part, :, :], AX.X, ALU.max).then_inc(max_done, 1)

            def rows_of_maxima(base, j, part, u):
                bank = filled(base, j)
                for h in range(2):
                    wrote = dve.tensor_tensor(T2m[u][h][0:NT, part * HALF:(part + 1) * HALF]
                                              .rearrange("t (a n) -> t a n", n=P),
                                              bank[0:NT, 0:P].rearrange("t (a n) -> t a n", a=1)
                                              .broadcast_to([NT, TPH, P]),
                                              diag[:, TPH * h:TPH * (h + 1)].rearrange("t (a n) -> t a n", n=1)
                                              .broadcast_to([NT, TPH, P]), ALU.mult)
                wrote.then_inc(m_used, 1)

            def invert(n):
                dve.wait_ge(cs_in, 32 * n)
                dve.reciprocal(rc[:, :, :], cs[:, :, :]).then_inc(inv_done, 1)

            def normalise(g, n, p):
                dve.wait_ge(rb_in, 32 * n)
                dve.wait_ge(o_used, 2 * g)
                sl = VS[:, bass.ds(p, 1), :]
                dve.tensor_tensor(sl, sl, rb[:, :].rearrange("p (a n) -> p a n", a=1), ALU.mult)\
                    .then_inc(norm_done, 1)

            dve.wait_ge(mod_in, 32)
            dve.wait_ge(exp_c, 1)
            dve.tensor_scalar(e_c[:, :], e_c[:, :], 1.0, None, ALU.add).then_inc(setup, 1)
            dve.wait_ge(setup, 1)
            dve.reciprocal(silu_c[:, :], e_c[:, :]).then_inc(setup, 1)
            dve.wait_ge(setup, 2)
            dve.tensor_tensor(silu_c[:, :], silu_c[:, :], c_sb[:, :], ALU.mult).then_inc(silu_done, 1)
            first_statistics(0)
            dve.wait_ge(mod_mm, 1)
            for n in range(3):
                dve.tensor_copy(modr[:, n * HALF:(n + 1) * HALF], MB[n][0:B, :]).then_inc(setup, 1)
            dve.tensor_copy(mod_t[:, 0:KD, :],
                            TB[0][:, 0:KD * B].rearrange("p (k b) -> p k b", b=B)).then_inc(setup, 1)
            dve.tensor_scalar(mod_t[:, KD:2 * KD, :],
                              TB[0][:, KD * B:2 * KD * B].rearrange("p (k b) -> p k b", b=B),
                              1.0, None, ALU.add).then_inc(setup, 1)
            dve.wait_ge(setup, 7)
            ca = modr[:, D:2 * D]
            dve.tensor_scalar(ca, ca, 1.0, None, ALU.add).then_inc(rows_done, 1)
            for n, m in enumerate((2, 5)):
                given, sign, size = modr[:, m * D:(m + 1) * D], guard[:, 2 * n, :], guard[:, 2 * n + 1, :]
                dve.tensor_scalar(size, given, -1.0, None, ALU.mult).then_inc(setup, 1)
                dve.tensor_scalar(sign, given, 0.0, 2.0, ALU.is_ge, ALU.mult).then_inc(setup, 1)
                dve.wait_ge(setup, 9 + 4 * n)
                dve.tensor_tensor(size, size, given, ALU.max).then_inc(setup, 1)
                dve.tensor_scalar(sign, sign, -1.0, None, ALU.add).then_inc(setup, 1)
                dve.wait_ge(setup, 11 + 4 * n)
                dve.scalar_tensor_tensor(out=given, in0=size, scalar=0.25, in1=sign, op0=ALU.max,
                                         op1=ALU.mult).then_inc(rows_done, 1)

            normalised(0, xt, hbuf)
            dve.wait_ge(x_in, 64)
            first_norm(0)
            second_norm(0)
            first_base(0)
            dve.wait_ge(const_in, 16 * LOADS)
            for n in range(6):
                rotate(n, 0)
            for n in range(4):
                low(n, 0, 0)
            for n in range(M_MAX):
                maxima(0, n, n)
            for part in range(2):
                rows_of_maxima(0, M_MAX + part, part, 0)

            with dve.Fori(0, B) as b:
                def step(g, p, u, prep, fin):
                    mb = m_base(b, p)
                    j = 0
                    for slot, what, n in step_order(prep, fin):
                        if what == "sum":
                            dve.tensor_copy(sums[:, n * HALF:(n + 1) * HALF], filled(mb, j)[:, :])\
                                .then_inc(m_used, 1)
                        elif what == "max2":
                            maxima(mb, j, M_MAX1 + n)
                            if not prep and n == 5:
                                first_statistics(b + 1)
                        elif what == "rows2":
                            rows_of_maxima(mb, j, 1, u)
                        elif what == "max1":
                            maxima(mb, j, n)
                        elif what == "rows1":
                            rows_of_maxima(mb, j, 0, 1 - u)
                        elif what == "rope":
                            rotate(n, g + 1)
                        elif what == "low":
                            low(n, g + 1, 1 - u)
                        elif what == "invert":
                            invert((NP - 1) * b + p)
                        else:
                            normalise(g, (NP - 1) * b + p, p - 1)
                        if slot is not None:
                            j += 1
                    if not prep:
                        first_norm(b + 1)
                        invert((NP - 1) * b + p)
                        second_norm(b + 1)
                        normalise(g, (NP - 1) * b + p, p - 1)

                steps(dve, b, step)
                dve.wait_ge(norm_done, (NP - 1 + NT // 2) * b + NP - 1)
                for w in range(NT // 2):
                    half, first = w // 2, w % 2 == 0
                    cols = slice(w * 2 * P, (w + 1) * 2 * P)
                    if first:
                        bank = filled(m_at(b, M_FIN), half)
                    inverse = dve.reciprocal(rb[:, cols], bank[:, w % 2 * 2 * P:(w % 2 + 1) * 2 * P])
                    if first:
                        inverse.then_inc(quarter_inv, 1)
                        dve.wait_ge(quarter_inv, 2 * b + half + 1)
                    else:
                        inverse.then_inc(m_used, 1)
                        dve.wait_ge(m_used, m_at(b, M_FIN + half + 1))
                    if w == 0:
                        dve.wait_ge(o_used, 16 * b + 2 * NP)
                    dve.tensor_tensor(VS[:, NP - 1, cols], VS[:, NP - 1, cols], rb[:, cols], ALU.mult)\
                        .then_inc(norm_done, 1)

                dve.tensor_copy(mod_c[:, :, :], mod_t[:, :, bass.ds(b, 1)]).then_inc(cols_done, 1)
                dve.wait_ge(base_in, 48 * b + 48)
                dve.wait_ge(rope_done, 16 * b + 16)
                mo = m_at(b, M_OUT)
                for w in range(NT // 2):
                    if w >= 2:
                        dve.wait_ge(x1_done, 4 * b + w - 1)
                    bank = filled(mo, w)
                    dve.tensor_tensor(obuf[:, w % 2, :, :], bank[:, :].rearrange("p (t d) -> p t d", d=D),
                                      row(mod_b, 0, 2), ALU.mult).then_inc(m_used, 1)
                    dve.wait_ge(m_used, mo + w + 1)
                    sl = xres[:, 2 * w:2 * w + 2, :]
                    dve.tensor_tensor(sl, sl, obuf[:, w % 2, :, :], ALU.add).then_inc(x1_done, 1)
                dve.wait_ge(x1_done, 4 * b + 4)
                statistics(3 * b + 4, xres)
                normalised(3 * b + 4, xres, n2buf)
                first_base(b + 1)

                dve.wait_ge(t_used, t_at(b, T_TR2 + T_TR))
                dve.tensor_scalar(sodd[:, :, :], h3T[:, :, 2:2 + 4 * LORA:2], ls_bc[:, 0:1], None, ALU.mult)\
                    .then_inc(odd_done, 1)
                for k in range(KD):
                    dve.tensor_tensor(D_sb[:, k, :, :],
                                      ident[:, :].rearrange("p (a n) -> p a n", a=1)
                                      .broadcast_to([P, 2 * LORA, P]),
                                      h3T[:, k, 1:1 + 4 * LORA:2].rearrange("p (a n) -> p a n", n=1)
                                      .broadcast_to([P, 2 * LORA, P]), ALU.mult).then_inc(spread_done, 1)
                dve.wait_ge(odd_done, b + 1)
                dve.wait_ge(wc_in, 32 * b + 32)

                for j in range(4):
                    second, k = j // 2, j % 2
                    bank = filled(m_at(b, M_LORA), j)
                    for i in range(LORA):
                        even = bank[:, i * P:(i + 1) * P]
                        for s in range(KD):
                            if second:
                                dst = w2_sb[:, s:NH:KD, 64 * i + 32 * k:64 * i + 32 * k + 32]
                                src = even.rearrange("p (a c) -> p c a", c=4)
                            else:
                                dst = w1_sb[:, s, D * i + P * k:D * i + P * (k + 1)]
                                src = even
                            last = dve.scalar_tensor_tensor(
                                out=dst, in0=src, scalar=sodd[:, s, LORA * second + i:LORA * second + i + 1],
                                in1=dst, op0=ALU.mult, op1=ALU.add)
                    last.then_inc(m_used, 1)
                    if j in (1, 2):
                        for n in range(3):
                            rotate(3 * (j - 1) + n, 8 * b + 8)
                for n in range(4):
                    low(n, 8 * b + 8, 0)

                mt = m_at(b, M_TAIL)
                dve.wait_ge(rope_done, 16 * b + 18)
                for j, (what, n) in enumerate(TAIL_UNITS):
                    if what == "ffn2":
                        o = obuf[:, n % 2, :, :]
                        if n >= 2:
                            dve.wait_ge(stored[n % 2], 16 + 32 * b + 16 * (n // 2))
                        bank = filled(mt, j)
                        dve.tensor_tensor(o, bank[:, :].rearrange("p (t d) -> p t d", d=D),
                                          b2_bc[:, :].rearrange("p (a d) -> p a d", a=1).broadcast_to([P, 2, D]),
                                          ALU.add).then_inc(m_used, 1)
                        dve.wait_ge(m_used, mt + j + 1)
                        dve.tensor_tensor(o, o, row(mod_b, 1, 2), ALU.mult).then_inc(gated, 1)
                        dve.wait_ge(gated, 4 * b + n + 1)
                        dve.tensor_tensor(o, o, xres[:, 2 * n:2 * n + 2, :], ALU.add).then_inc(out_ready, 1)
                    elif what == "max":
                        maxima(mt, j, n)
                    else:
                        rows_of_maxima(mt, j, n, 0)


def kernel(**inputs):
    import numpy as np
    import concourse.bacc as bacc
    from concourse.bass_utils import run_bass_kernel_spmd

    a = {n.removeprefix("L0_"): np.asarray(v) for n, v in inputs.items()}

    inv_freq = 1.0 / 10000.0 ** (np.arange(0, DH, 2, dtype=np.float32) / DH)
    freqs = np.outer(np.arange(S, dtype=np.float32), inv_freq)
    cos = np.concatenate([np.cos(freqs), np.cos(freqs)], -1)[:, ::2].T
    sin = np.concatenate([np.sin(freqs), np.sin(freqs)], -1)[:, ::2].T
    signed = np.stack([-sin, sin], 1)
    rope = np.stack([np.tile(np.repeat(cos, 2, 0), (2, 1)),
                     np.tile(signed.reshape(DH, S), (2, 1))], 1).astype(np.float32)

    def pairs(w):
        return w.reshape(NP, P, R).transpose(0, 2, 1)

    def tiles(w):
        return w.reshape(-1, P, w.shape[1]).transpose(1, 0, 2)

    wq, wk = a["attn_w_up_q"], a["attn_w_up_k"]
    arrays = {
        "x": a["attn_x"],
        "w_pair": np.stack([pairs(wq), pairs(wk)], 2),
        "w_v": a["attn_w_up_v"].T,
        "w_down": np.stack([tiles(a["attn_w_down_q"].T), tiles(a["attn_w_down_kv"].T)], 2),
        "w_out": tiles(a["attn_w_out"].T),
        "w1": tiles(a["ffn_W1"].T),
        "w2": tiles(a["ffn_W2"].T),
        "ln_cols": np.concatenate([a["attn_ln_scale"].reshape(KD, P), a["attn_ln_bias"].reshape(KD, P)]).T,
        "b1_cols": a["ffn_b1"].reshape(NH, P).T,
        "b2": a["ffn_b2"].reshape(1, D),
        "lora_scale": a["ffn_scale"].reshape(1, 1),
        "c_cols": tiles(a["c"].T).reshape(P, KD * B),
        "w_mod": tiles(a["wmod"]),
        "rope": rope,
        "ident_in": np.eye(P, dtype=np.float32),
        "diag_in": -np.eye(NT, dtype=np.float32),
    }
    nc = bacc.Bacc("TRN2", target_bir_lowering=False, num_devices=1)
    args, sent = {}, {}
    for name, v in arrays.items():
        v = np.ascontiguousarray(v)
        sent[f"in_{name}"] = v
        args[name] = nc.dram_tensor(f"in_{name}", v.shape, mybir.dt.from_np(v.dtype), kind="ExternalInput").ap()
    args["out"] = nc.dram_tensor("out_0", (B, S, D), mybir.dt.float32, kind="ExternalOutput").ap()
    build(nc, **args)
    return run_bass_kernel_spmd(nc, [sent], core_ids=[0]).results[0]["out_0"]
```
